# Optimizing a Trainium2 kernel written in Bass

```python
import numpy as np
import jax
import jax.numpy as jnp

def _softmax(x, axis=-1):
    return jax.nn.softmax(x, axis=axis)

def _gelu(x):
    return jax.nn.gelu(x, approximate=True)

def _silu(x):
    return jax.nn.silu(x)

def _sigmoid(x):
    return jax.nn.sigmoid(x)

def _layernorm(x, axis=-1, eps=1e-05):
    m = jnp.mean(x, axis=axis, keepdims=True)
    v = jnp.var(x, axis=axis, keepdims=True)
    return (x - m) / jnp.sqrt(v + eps)

def _scatter_add(tgt, idx, src, axis=0):
    return tgt.at[idx].add(src)

def _segment_sum(src, seg, n):
    return jax.ops.segment_sum(src, seg, n)
kernel_name = 'mk_recurrent_d1_jaxref_r8_0bddac'

def setup_inputs(seed: int=0):
    np.random.seed(seed)
    _w = jnp.asarray

    def _L0_attn_setup():
        import jax, jax.numpy as jnp
        import numpy as np
        DIM = 256
        HEADS = 32
        WINDOW = 8
        B = 4
        N = 197

        def _local_mask(w, n):
            i = jnp.arange(n)[:, None]
            j = jnp.arange(n)[None, :]
            d = jnp.abs(i - j).astype(jnp.float32)
            in_win = (j >= i - w) & (j < i + w)
            return jnp.where(in_win, (w - d / 2.0) / w, 0.0)
        key = jax.random.key(seed)
        k1, k2, k3, k4 = jax.random.split(key, 4)
        x = jax.random.normal(k1, (B, N, DIM), dtype=jnp.float32)
        qkv_w = jax.random.normal(k2, (3 * DIM, DIM), dtype=jnp.float32) * 0.02
        proj_w = jax.random.normal(k3, (DIM, DIM), dtype=jnp.float32) * 0.02
        proj_b = jax.random.normal(k4, (DIM,), dtype=jnp.float32) * 0.02
        return {'x': x, 'qkv_w': qkv_w, 'proj_w': proj_w, 'proj_b': proj_b}
    _L0_attn_in = _L0_attn_setup()

    def _L0_ffn_setup():
        import jax, jax.numpy as jnp
        import numpy as np
        SEQ, BS, D, F, E = (128, 2, 256, 256, 8)
        key = jax.random.key(seed)
        ks = jax.random.split(key, 8)
        s = 0.02
        return {'hidden_states': jax.random.normal(ks[0], (SEQ, BS, D), jnp.float32), 'router_w': jax.random.normal(ks[1], (D, E), jnp.float32) * s, 'gate_w': jax.random.normal(ks[2], (E, D, F), jnp.float32) * s, 'up_w': jax.random.normal(ks[3], (E, D, F), jnp.float32) * s, 'down_w': jax.random.normal(ks[4], (E, F, D), jnp.float32) * s, 'shared_gate_w': jax.random.normal(ks[5], (D, F), jnp.float32) * s, 'shared_up_w': jax.random.normal(ks[6], (D, F), jnp.float32) * s, 'shared_down_w': jax.random.normal(ks[7], (F, D), jnp.float32) * s}
    _L0_ffn_in = _L0_ffn_setup()
    _d = {'L0_attn_x': _L0_attn_in['x'], 'L0_attn_qkv_w': _L0_attn_in['qkv_w'], 'L0_attn_proj_w': _L0_attn_in['proj_w'], 'L0_attn_proj_b': _L0_attn_in['proj_b'], 'L0_ffn_router_w': _L0_ffn_in['router_w'], 'L0_ffn_gate_w': _L0_ffn_in['gate_w'], 'L0_ffn_up_w': _L0_ffn_in['up_w'], 'L0_ffn_down_w': _L0_ffn_in['down_w'], 'L0_ffn_shared_gate_w': _L0_ffn_in['shared_gate_w'], 'L0_ffn_shared_up_w': _L0_ffn_in['shared_up_w'], 'L0_ffn_shared_down_w': _L0_ffn_in['shared_down_w']}
    _x0 = _d['L0_attn_x']
    _d['L0_attn_x'] = jax.random.normal(jax.random.fold_in(jax.random.key(seed), 1), (8, 512, 256), dtype=_x0.dtype)
    del _x0
    return _d

def reference(L0_attn_x, L0_attn_qkv_w, L0_attn_proj_w, L0_attn_proj_b, L0_ffn_router_w, L0_ffn_gate_w, L0_ffn_up_w, L0_ffn_down_w, L0_ffn_shared_gate_w, L0_ffn_shared_up_w, L0_ffn_shared_down_w):

    def _L0_attn_ref(x, qkv_w, proj_w, proj_b):
        import jax, jax.numpy as jnp
        import numpy as np
        DIM = 256
        HEADS = 32
        WINDOW = 8
        B = 4
        N = 197

        def _local_mask(w, n):
            i = jnp.arange(n)[:, None]
            j = jnp.arange(n)[None, :]
            d = jnp.abs(i - j).astype(jnp.float32)
            in_win = (j >= i - w) & (j < i + w)
            return jnp.where(in_win, (w - d / 2.0) / w, 0.0)
        Bb, Nn, C = x.shape
        H = HEADS
        hd = C // H
        scale = hd ** (-0.5)
        qkv = (x @ qkv_w.T).reshape(Bb, Nn, 3, H, hd).transpose(2, 0, 3, 1, 4)
        q, k, v = (qkv[0], qkv[1], qkv[2])
        attn = jnp.einsum('bhnd,bhmd->bhnm', q, k) * scale
        m = _local_mask(WINDOW, Nn)
        attn = jnp.where(m != 0.0, attn * m, -jnp.inf)
        attn = jax.nn.softmax(attn, axis=-1)
        out = jnp.einsum('bhnm,bhmd->bhnd', attn, v)
        out = out.transpose(0, 2, 1, 3).reshape(Bb, Nn, C)
        return out @ proj_w.T + proj_b

    def _L0_ffn_ref(hidden_states, router_w, gate_w, up_w, down_w, shared_gate_w, shared_up_w, shared_down_w):
        import jax, jax.numpy as jnp
        import numpy as np
        SEQ, BS, D, F, E = (128, 2, 256, 256, 8)
        S, B, Dm = hidden_states.shape
        x = hidden_states.reshape(-1, Dm)
        logits = x @ router_w
        expert_idx = jnp.argmax(logits, axis=-1)
        score = jax.nn.sigmoid(jnp.max(logits, axis=-1))
        xs = x * score[:, None]
        n_experts = router_w.shape[1]
        out = jnp.zeros_like(x)
        for e in range(n_experts):
            m = (expert_idx == e)[:, None]
            xe = jnp.where(m, xs, 0.0)
            h = jax.nn.silu(xe @ gate_w[e]) * (xe @ up_w[e])
            out = out + jnp.where(m, h @ down_w[e], 0.0)
        shared = jax.nn.silu(x @ shared_gate_w) * (x @ shared_up_w) @ shared_down_w
        return (out + shared).reshape(S, B, Dm)
    x = L0_attn_x
    xn = _layernorm(x, axis=-1)
    s = _L0_attn_ref(xn, L0_attn_qkv_w, L0_attn_proj_w, L0_attn_proj_b)
    g = _silu(_L0_ffn_ref(xn, L0_ffn_router_w, L0_ffn_gate_w, L0_ffn_up_w, L0_ffn_down_w, L0_ffn_shared_gate_w, L0_ffn_shared_up_w, L0_ffn_shared_down_w))
    x = x + s * g
    return x

_drawn_inputs = setup_inputs


def setup_inputs(seed=0):
    import zlib

    import numpy as np

    out = dict(_drawn_inputs(seed))
    spreads = {}
    factors = {'L0_attn_qkv_w': 8.0,
     'L0_attn_proj_w': 8.0,
     'L0_attn_proj_b': 8.0,
     'L0_ffn_router_w': 8.0,
     'L0_ffn_gate_w': 8.0,
     'L0_ffn_up_w': 8.0,
     'L0_ffn_down_w': 8.0,
     'L0_ffn_shared_gate_w': 8.0,
     'L0_ffn_shared_up_w': 8.0,
     'L0_ffn_shared_down_w': 8.0}
    for name, (base, spread) in spreads.items():
        noise = np.random.default_rng([zlib.crc32(name.encode()), seed]).standard_normal(out[name].shape)
        drawn = base * np.exp(spread * noise) if base else spread * noise
        out[name] = jnp.asarray(drawn.astype(out[name].dtype))
    for name, factor in factors.items():
        out[name] = (out[name] * factor).astype(out[name].dtype)
    return out
```

```python
from contextlib import ExitStack

import numpy as np

import concourse.bass as bass
from concourse import mybir

F32 = mybir.dt.float32
I32 = mybir.dt.int32
U32 = mybir.dt.uint32
ALU = mybir.AluOpType
ACT = mybir.ActivationFunctionType
AX = mybir.AxisListType.X

P = 128
BATCH, SEQ, C = 8, 512, 256
H, HD = 32, 8
WIN = 8
NJ = 2 * WIN
E, F = 8, 256
T = BATCH * SEQ // P
SEGS = SEQ // T
KC = C // P
HALO_L, HALO_R = WIN, WIN - 1
NPOS = T + HALO_L + HALO_R
NT = T + E
EPS = 1e-5
NEG = -3e38
WEXP = KC * 2 * F + KC * C
POOL_J = 11

C_ID, C_TRI, C_ONE = 0, P, 2 * P
C_WJ = 3 * P
C_EDGE = C_WJ + NJ * H
C_FIRST = C_EDGE + 2
C_TILE = C_FIRST + E
C_END = C_TILE + NT


def constants():
    c = np.zeros((P, C_END), np.float32)
    c[:, C_ID:C_ID + P] = np.eye(P)
    c[:, C_TRI:C_TRI + P] = np.triu(np.ones((P, P)), 1)
    c[:, C_ONE:C_ONE + P] = 1.0
    d = np.abs(np.arange(NJ) - WIN).astype(np.float32)
    c[:, C_WJ:C_WJ + NJ * H] = np.repeat((WIN - d / 2.0) / WIN * np.float32(HD ** -0.5), H)
    p = np.arange(P)
    c[:, C_EDGE] = np.where(p % SEGS == 0, NEG, 0.0)
    c[:, C_EDGE + 1] = np.where(p % SEGS == SEGS - 1, NEG, 0.0)
    c[:, C_FIRST:C_FIRST + E] = E - np.arange(E)
    c[:, C_TILE:C_TILE + NT] = np.arange(NT)
    return c


def by_tile(eng, n, body):
    body(0, 0)
    body(1, 1)
    with eng.Fori(1, n // 2 - 1) as pair:
        body(pair * 2, 0)
        body(pair * 2 + 1, 1)
    body(n - 2, 0)
    body(n - 1, 1)


def static(t):
    return isinstance(t, int)


def wait_turn(eng, sem, t):
    eng.wait_ge(sem, (t // 2) * 16 + 16)


def wait_before(eng, sem, t):
    eng.wait_ge(sem, (t // 2) * 16)


def build(nc, x, qkv_w, proj_w, proj_b, router_w, gate_w, up_w, down_w, sgate_w, sup_w, sdown_w,
          const, out, q_dram, shared_dram, xs_dram, ys_dram):
    ctx = ExitStack()
    with ctx:
        def sb(name, shape, dt=F32):
            return ctx.enter_context(nc.sbuf_tensor(name, shape, dt))

        def sem(name):
            return ctx.enter_context(nc.semaphore(name))

        K = sb("K", [P, NPOS, C])
        V = sb("V", [P, NPOS, C])
        R = sb("R", [P, E * WEXP])
        cst = sb("cst", [P, C_END])
        wt = sb("wt", [P, KC, 4 * C])
        wgu = sb("wgu", [P, KC, 2 * F])
        wdn = sb("wdn", [P, KC, C])
        wrt = sb("wrt", [P, KC, E])
        pbias = sb("pbias", [P, C])
        xnb = sb("xnb", [P, 2, C])
        xT = sb("xT", [P, 2, C])
        hb = sb("hb", [P, 2, C])
        hT = sb("hT", [P, 2, C])
        ga = sb("ga", [P, 2, C])
        gr = sb("gr", [P, 2, C])
        stage = sb("stage", [P, 4, C])
        tin = sb("tin", [P, 2, 3, C])
        small = sb("small", [P, 2, NJ * H])
        mx = sb("mx", [P, 2, H])
        stats = sb("stats", [P, T, 6])
        mv = sb("mv", [P, 8, T])
        lg = sb("lg", [P, T, E])
        rt = sb("rt", [P, 4, T * E])
        cnt = sb("cnt", [P, 8, E])
        cnti = sb("cnti", [P, E], I32)
        slot = sb("slot", [P, T], U32)
        idx = sb("idx", [P, 4], U32)
        etab = sb("etab", [P, NT, E])
        etabs = sb("etabs", [P, NT])
        etabi = sb("etabi", [P, NT], I32)

        ident = cst[:, C_ID:C_ID + P]
        tri = cst[:, C_TRI:C_TRI + P]
        ones = cst[:, C_ONE:C_ONE + P]
        wj = cst[:, C_WJ:C_WJ + NJ * H]
        XO = 4096
        X = R[:, XO:XO + T * C].rearrange("p (t c) -> p t c", c=C)
        raw = K[:, 0:8, :]
        prodA = [R[:, i * NJ * C:(i + 1) * NJ * C].rearrange("p (j c) -> p j c", c=C) for i in range(2)]
        prodB = R[:, 2 * NJ * C:3 * NJ * C].rearrange("p (j c) -> p j c", c=C)

        ps = [ctx.enter_context(nc.psum_tensor(f"ps{i}", [P, 512], F32)) for i in range(8)]

        s_const, s_raw, s_w, s_zero, s_fill = (sem(n) for n in ("s_const", "s_raw", "s_w", "s_zero", "s_fill"))
        s_x = [sem(f"s_x{i}") for i in range(4)]
        s_wtp, s_wtc = sem("s_wtp"), sem("s_wtc")
        s_dve = sem("s_dve")
        s_bn = sem("s_bn")
        s_var, s_sqrt = sem("s_var"), sem("s_sqrt")
        a_xn, a_xTp, a_xT, a_qk, a_vr, a_gu = (sem("a_" + n) for n in ("xn", "xTp", "xT", "qk", "vr", "gu"))
        a_exp, a_h, a_hTp, a_hT, a_dn, a_lg = (sem("a_" + n) for n in ("exp", "h", "hTp", "hT", "dn", "lg"))
        a_q, a_kv, a_sh = (sem("a_" + n) for n in ("q", "kv", "sh"))
        a_qst, a_sst = ([sem(f"a_{n}{i}") for i in range(2)] for n in ("qst", "sst"))
        b_oh, b_cnt, b_sc, b_tab, b_row, b_halo, b_w0, b_w1 = (
            sem("b_" + n) for n in ("oh", "cnt", "sc", "tab", "row", "halo", "w0", "w1"))
        b_sce = sem("b_sce")
        b_scat = [sem(f"b_scat{k}") for k in range(4)]
        b_in = [sem(f"b_in{i}") for i in range(2)]
        b_st = [sem(f"b_st{i}") for i in range(2)]
        b_xTp, b_xT, b_gu, b_exp, b_h, b_hTp, b_hT, b_dn, b_y = (
            sem("b_" + n) for n in ("xTp", "xT", "gu", "exp", "h", "hTp", "hT", "dn", "y"))
        c_ld = [sem(f"c_ld{i}") for i in range(2)]
        c_q = [sem(f"c_q{i}") for i in range(2)]
        c_g = [sem(f"c_g{i}") for i in range(2)]
        c_idx, c_pa, c_pb, c_s, c_e, c_pbd, c_red, c_sum = (
            sem("c_" + n) for n in ("idx", "pa", "pb", "s", "e", "pbd", "red", "sum"))
        c_on, c_oTp, c_oT, c_pr, c_f, c_fe, c_out = (
            sem("c_" + n) for n in ("on", "oTp", "oT", "pr", "f", "fe", "out"))
        c_st = [sem(f"c_st{i}") for i in range(2)]

        wexp = R[:, :].rearrange("p (e w) -> p e w", w=WEXP)

        def load_experts(eng, lo, hi, s):
            n = 0
            for e in range(lo, hi):
                g = wexp[:, e, 0:KC * 2 * F].rearrange("p (k f) -> p k f", k=KC)
                for w, c0 in ((gate_w, 0), (up_w, F)):
                    eng.dma_start(g[:, :, c0:c0 + F], w[e].rearrange("(k p) f -> p k f", p=P)).then_inc(s, 16)
                eng.dma_start(wexp[:, e, KC * 2 * F:WEXP].rearrange("p (k c) -> p k c", k=KC),
                              down_w[e].rearrange("(k p) c -> p k c", p=P)).then_inc(s, 16)
                n += 3
            return 16 * n

        E0 = XO // WEXP
        x_v = x.rearrange("(p t) c -> p t c", t=T)
        out_v = out.rearrange("(p t) c -> p t c", t=T)
        XCH = 4
        BA = 8
        BB = 3
        block = ctx.enter_context(nc.Block())

        @block.sync
        def _(sp):
            sp.dma_start(cst[:, :], const).then_inc(s_const, 16)
            n = T // XCH
            for i in range(XCH):
                sp.dma_start(X[:, i * n:(i + 1) * n, :], x_v[:, i * n:(i + 1) * n, :]).then_inc(s_x[i], 16)
            sp.dma_start(raw[:, 0:6, :], qkv_w.rearrange("(a p) c -> p a c", p=P)).then_inc(s_raw, 16)
            sp.dma_start(raw[:, 6:8, :], proj_w.rearrange("(a p) c -> p a c", p=P)).then_inc(s_raw, 16)
            for dst, src in ((wgu[:, :, 0:F], sgate_w), (wgu[:, :, F:2 * F], sup_w), (wdn[:, :, :], sdown_w),
                             (wrt[:, :, :], router_w)):
                sp.dma_start(dst, src.rearrange("(k p) f -> p k f", p=P)).then_inc(s_w, 16)
            sp.dma_start(pbias[:, :], proj_b.unsqueeze(0).broadcast_to([P, C])).then_inc(s_w, 16)
            load_experts(sp, 0, E0, b_w0)
            sp.wait_ge(s_zero, 1)
            for i in range(NT // 4):
                sp.dma_start(xs_dram[i * 4 * P:(i + 1) * 4 * P, :].rearrange("(p r) c -> p r c", r=4),
                             stage[:, :, :]).then_inc(s_fill, 16)

            def save(r, u):
                sp.wait_ge(a_q, r + 1)
                sp.dma_start(q_dram[:, bass.ds(r, 1), :], small[:, u:u + 1, 0:C]).then_inc(a_qst[u], 16)
                sp.wait_ge(a_sh, r + 1)
                sp.dma_start(shared_dram[:, bass.ds(r, 1), :], tin[:, u, 0:1, :]).then_inc(a_sst[u], 16)
            by_tile(sp, T, save)

            sp.wait_ge(a_kv, T)
            for t in (K, V):
                sp.dma_start(t[1:P, 0:HALO_L, :], t[0:P - 1, T:T + HALO_L, :]).then_inc(b_halo, 16)
                sp.dma_start(t[0:1, 0:HALO_L, :], t[0:1, T:T + HALO_L, :]).then_inc(b_halo, 16)
                sp.dma_start(t[0:P - 1, HALO_L + T:NPOS, :], t[1:P, HALO_L:HALO_L + HALO_R, :]).then_inc(b_halo, 16)
                sp.dma_start(t[P - 1:P, HALO_L + T:NPOS, :], t[P - 1:P, HALO_L:HALO_L + HALO_R, :]).then_inc(b_halo, 16)

            sp.wait_ge(b_row, T)
            for k in range(4):
                sp.wait_ge(b_scat[k], 16 * (T // 4))
            load_experts(sp, E0, E, b_w1)

            def rows(i, u):
                if static(i) and i < 2:
                    pass
                else:
                    sp.wait_ge(b_xTp, i - 1)
                sp.dma_start(xnb[:, u, :], xs_dram[bass.ds(i * P, P), :]).then_inc(b_in[u], 16)
                if not (static(i) and i < 2):
                    store(i - 2, u)

            def store(i, u):
                sp.wait_ge(b_y, i + 1)
                sp.dma_start(ys_dram[bass.ds(i * P, P), :], tin[:, u, 0, :]).then_inc(b_st[u], 16)
            by_tile(sp, NT, rows)
            store(NT - 2, 0)
            store(NT - 1, 1)

            for u in range(2):
                sp.wait_ge(a_qst[u], 8 * T)
                sp.wait_ge(a_sst[u], 8 * T)
            for u in range(2):
                sp.wait_ge(b_st[u], 8 * NT)

            def loads(r, u):
                if not (static(r) and r < 2):
                    sp.wait_ge(c_pa, 2 * r - 2)
                sp.dma_start(xnb[:, u:u + 1, :], q_dram[:, bass.ds(r, 1), :]).then_inc(c_q[u], 16)
                if not (static(r) and r < 2):
                    store_out(r - 2, u)
                sp.dma_start(tin[:, u, 0:1, :], x_v[:, bass.ds(r, 1), :]).then_inc(c_ld[u], 16)
                sp.dma_start(tin[:, u, 1:2, :], shared_dram[:, bass.ds(r, 1), :]).then_inc(c_ld[u], 16)

            def store_out(r, u):
                sp.wait_ge(c_out, r + 1)
                sp.dma_start(out_v[:, bass.ds(r, 1), :], gr[:, u:u + 1, :]).then_inc(c_st[u], 16)
            sp.wait_ge(b_xTp, NT)
            by_tile(sp, T, loads)
            store_out(T - 2, 0)
            store_out(T - 1, 1)
            for u in range(2):
                sp.wait_ge(c_st[u], 8 * T)

        @block.gpsimd
        def _(pool):
            nc.gpsimd.memset(stage[:, :, :], 0.0).then_inc(s_zero, 1)
            pool.wait_ge(s_const, 16)
            pool.wait_ge(s_fill, 16 * (NT // 4))

            for q in range(T // 4):
                for k in range(4):
                    pool.wait_ge(b_row, q * 4 + k + 1)
                    pool.indirect_dma_start(xs_dram, bass.IndirectOffsetOnAxis(ap=idx[:, k:k + 1], axis=0),
                                            stage[:, k, :], None).then_inc(b_scat[k], 16)
            pool.wait_ge(b_halo, 16 * 8)
            for u in range(2):
                pool.wait_ge(b_st[u], 8 * NT)

            def keys(r, u):
                wait_turn(pool, c_q[u], r)
                if not (static(r) and r < 2):
                    pool.wait_ge(c_red, r - 1)
                nc.gpsimd.tensor_tensor(
                    prodA[u][:, 0:POOL_J, :], K[:, bass.ds(r, POOL_J), :],
                    xnb[:, u, :].unsqueeze(1).broadcast_to([P, POOL_J, C]), ALU.mult).then_inc(c_pa, 1)

            def gather(r, u):
                pool.indirect_dma_start(tin[:, u, 2, :], None, ys_dram,
                                        bass.IndirectOffsetOnAxis(ap=idx[:, u:u + 1], axis=0)).then_inc(c_g[u], 16)

            def values(r, u):
                pool.wait_ge(c_e, r + 1)
                if not (static(r) and r < 1):
                    pool.wait_ge(c_sum, r)
                nc.gpsimd.tensor_tensor(
                    prodB[:, 0:POOL_J, :].rearrange("p j (h d) -> p j h d", d=HD),
                    V[:, bass.ds(r, POOL_J), :].rearrange("p j (h d) -> p j h d", d=HD),
                    small[:, u, 0:POOL_J * H].rearrange("p (j h) -> p j h", h=H).unsqueeze(3)
                    .broadcast_to([P, POOL_J, H, HD]), ALU.mult).then_inc(c_pb, 1)
            keys(0, 0)

            def tile(r, u):
                pool.wait_ge(c_idx, r + 1)
                if not (static(r) and r == T - 1):
                    keys(r + 1, 1 - u)
                gather(r, u)
                values(r, u)
            by_tile(pool, T, tile)

        @block.scalar
        def _(act):
            act.wait_ge(s_var, 1)
            nc.scalar.activation(mv[:, 2, :], mv[:, 1, :], ACT.Sqrt).then_inc(s_sqrt, 1)
            for b in range(4):
                act.wait_ge(s_wtp, b + 1)
                nc.scalar.activation(wt[:, b // 2, 512 * (b % 2):512 * (b % 2) + 512], ps[b][:, :],
                                     ACT.Copy).then_inc(s_wtc, 1)

            def xcopy(r, u):
                act.wait_ge(a_xTp, r + 1)
                if not (static(r) and r < 2):
                    act.wait_ge(a_gu, r - 1)
                nc.scalar.activation(xT[:, u, :], ps[u][:, 0:C], ACT.Copy).then_inc(a_xT, 1)

            def a_tile(r, u):
                if static(r) and r == 0:
                    xcopy(0, 0)
                if not (static(r) and r == T - 1):
                    xcopy(r + 1, 1 - u)
                act.wait_ge(a_qk, r + 1)
                if not (static(r) and r < 2):
                    wait_before(act, a_qst[u], r)
                nc.scalar.activation(small[:, u, 0:C], ps[2 + u][:, 0:C], ACT.Copy).then_inc(a_q, 1)
                nc.scalar.activation(K[:, bass.ds(r + HALO_L, 1), :], ps[2 + u][:, C:2 * C].unsqueeze(1), ACT.Copy)
                act.wait_ge(a_vr, r + 1)
                act.wait_ge(a_lg, r + 1)
                nc.scalar.activation(V[:, bass.ds(r + HALO_L, 1), :], ps[4][:, 0:C].unsqueeze(1), ACT.Copy).then_inc(a_kv, 1)
                act.wait_ge(a_gu, r + 1)
                if not (static(r) and r < 2):
                    act.wait_ge(a_h, r - 1)
                nc.scalar.activation(ga[:, u, :], ps[5][:, 0:F], ACT.Exp, scale=-1.0).then_inc(a_exp, 1)
                if not (static(r) and r == 0):
                    a_down(r - 1, 1 - u)

            def a_down(r, u):
                act.wait_ge(a_hTp, r + 1)
                nc.scalar.activation(hT[:, u, :], ps[6][:, 0:F], ACT.Copy).then_inc(a_hT, 1)
                act.wait_ge(a_dn, r + 1)
                if not (static(r) and r < 2):
                    wait_before(act, a_sst[u], r)
                nc.scalar.activation(tin[:, u, 0, :], ps[7][:, 0:C], ACT.Copy).then_inc(a_sh, 1)
            by_tile(act, T, a_tile)
            a_down(T - 1, 1)

            act.wait_ge(b_sc, 1)
            nc.scalar.activation(mv[:, 5, :], mv[:, 4, :], ACT.Exp, scale=-1.0).then_inc(b_sce, 1)
            for u in range(2):
                act.wait_ge(a_sst[u], 8 * T)

            def b_xcopy(i, u):
                act.wait_ge(b_xTp, i + 1)
                if not (static(i) and i < 2):
                    act.wait_ge(b_gu, i - 1)
                nc.scalar.activation(xT[:, u, :], ps[u][:, 0:C], ACT.Copy).then_inc(b_xT, 1)

            def b_tile(i, u):
                if static(i) and i == 0:
                    b_xcopy(0, 0)
                if not (static(i) and i == NT - 1):
                    b_xcopy(i + 1, 1 - u)
                act.wait_ge(b_gu, i + 1)
                if not (static(i) and i < 2):
                    act.wait_ge(b_h, i - 1)
                nc.scalar.activation(ga[:, u, :], ps[2 + u][:, 0:F], ACT.Exp, scale=-1.0).then_inc(b_exp, 1)
                if not (static(i) and i == 0):
                    b_down(i - 1, 1 - u)

            def b_down(i, u):
                act.wait_ge(b_hTp, i + 1)
                nc.scalar.activation(hT[:, u, :], ps[4 + u][:, 0:F], ACT.Copy).then_inc(b_hT, 1)
                act.wait_ge(b_dn, i + 1)
                if not (static(i) and i < 2):
                    wait_before(act, b_st[u], i)
                nc.scalar.activation(tin[:, u, 0, :], ps[6 + u][:, 0:C], ACT.Copy).then_inc(b_y, 1)
            by_tile(act, NT, b_tile)
            b_down(NT - 1, 1)

            def c_tile(r, u):
                act.wait_ge(c_s, r + 1)
                nc.scalar.activation(small[:, u, :], small[:, u, :], ACT.Exp).then_inc(c_e, 1)
                act.wait_ge(c_f, r + 1)
                nc.scalar.activation(ga[:, u, :], gr[:, u, :], ACT.Exp, scale=-1.0).then_inc(c_fe, 1)
                if not (static(r) and r == 0):
                    c_proj(r - 1, 1 - u)

            def c_proj(r, u):
                act.wait_ge(c_oTp, r + 1)
                nc.scalar.activation(hT[:, u, :], ps[2][:, 0:C], ACT.Copy).then_inc(c_oT, 1)
            by_tile(act, T, c_tile)
            c_proj(T - 1, 1)

        @block.vector
        def _(dve):
            def chain(base):
                n = [0]

                def step(ins):
                    n[0] += 1
                    ins.then_inc(s_dve, 1)
                    dve.wait_ge(s_dve, base + n[0])
                return step, n
            tt, ts = nc.vector.tensor_tensor, nc.vector.tensor_scalar
            n = T // XCH
            for i in range(XCH):
                dve.wait_ge(s_x[i], 16)
                with dve.Fori(i * n, (i + 1) * n) as t:
                    nc.vector.bn_stats(stats[:, bass.ds(t, 1), :], X[:, bass.ds(t, 1), :]).then_inc(s_bn, 1)
            dve.wait_ge(s_const, 16)
            dve.wait_ge(s_bn, T)
            step, at = chain(0)
            me, m2e, mo, m2o = (stats[:, :, k] for k in (1, 2, 4, 5))
            step(ts(mv[:, 7, :], me, 0.0, None, ALU.add))
            step(tt(mv[:, 0, :], mv[:, 7, :], mo, ALU.add))
            step(tt(mv[:, 3, :], me, mo, ALU.subtract))
            step(tt(mv[:, 4, :], m2e, m2o, ALU.add))
            step(tt(mv[:, 3, :], mv[:, 3, :], mv[:, 3, :], ALU.mult))
            step(ts(mv[:, 4, :], mv[:, 4, :], 1.0 / C, EPS, ALU.mult, ALU.add))
            step(ts(mv[:, 0, :], mv[:, 0, :], 0.5, None, ALU.mult))
            step(ts(mv[:, 3, :], mv[:, 3, :], 0.25, None, ALU.mult))
            step(tt(mv[:, 1, :], mv[:, 3, :], mv[:, 4, :], ALU.add))
            nc.vector.tensor_copy(mv[:, 7, :], mv[:, 1, :]).then_inc(s_var, 1)
            dve.wait_ge(s_sqrt, 1)
            step(nc.vector.reciprocal(mv[:, 3, :], mv[:, 2, :]))
            step(tt(mv[:, 3, :], mv[:, 3, :], mv[:, 1, :], ALU.mult))
            step(tt(mv[:, 3, :], mv[:, 3, :], mv[:, 2, :], ALU.add))
            step(ts(mv[:, 3, :], mv[:, 3, :], 0.5, None, ALU.mult))
            step(nc.vector.reciprocal(mv[:, 6, :], mv[:, 3, :]))
            base_a = at[0]

            def norm(r, u):
                if not (static(r) and r < 2):
                    dve.wait_ge(a_xTp, r - 1)
                a = (X[:, bass.ds(r, 1), :], mv[:, 0, bass.ds(r, 1)], mv[:, 6, bass.ds(r, 1)], ALU.subtract, ALU.mult)
                ts(xnb[:, u:u + 1, :], *a).then_inc(a_xn, 1)
                ts(X[:, bass.ds(r, 1), :], *a)

            def swiglu(r, u, step, gu, s_gu, s_exp, s_h, free):
                dve.wait_ge(s_exp, r + 1)
                step(ts(ga[:, u, :], ga[:, u, :], 1.0, None, ALU.add))
                step(nc.vector.reciprocal(gr[:, u, :], ga[:, u, :]))
                step(tt(gr[:, u, :], gu[:, 0:F], gr[:, u, :], ALU.mult))
                if not (static(r) and r < 2):
                    dve.wait_ge(free, r - 1)
                tt(hb[:, u, :], gu[:, F:2 * F], gr[:, u, :], ALU.mult).then_inc(s_h, 1)

            def a_tile(r, u):
                if static(r) and r == 0:
                    norm(0, 0)
                if not (static(r) and r == T - 1):
                    norm(r + 1, 1 - u)
                dve.wait_ge(a_vr, r + 1)
                nc.vector.tensor_copy(lg[:, bass.ds(r, 1), :], ps[4][:, C:C + E].unsqueeze(1)).then_inc(a_lg, 1)
                step, _ = chain(r * BB + base_a)
                swiglu(r, u, step, ps[5], a_gu, a_exp, a_h, a_hTp)
            by_tile(dve, T, a_tile)

            step, at = chain(base_a + BB * T)
            dve.wait_ge(a_lg, T)
            v3 = lambda k: rt[:, k, :].rearrange("p (t e) -> p t e", e=E)
            step(nc.vector.tensor_reduce(mv[:, 4, :], lg[:, :, :], AX, ALU.max))
            nc.vector.tensor_copy(mv[:, 7, :], mv[:, 4, :]).then_inc(b_sc, 1)
            step(tt(v3(0), lg[:, :, :], mv[:, 4, :].unsqueeze(2).broadcast_to([P, T, E]), ALU.is_ge))
            first = cst[:, C_FIRST:C_FIRST + E].unsqueeze(1).broadcast_to([P, T, E])
            step(tt(v3(0), v3(0), first, ALU.mult))
            step(nc.vector.tensor_reduce(mv[:, 3, :], v3(0), AX, ALU.max))
            nc.vector.tensor_tensor(v3(1), first, mv[:, 3, :].unsqueeze(2).broadcast_to([P, T, E]),
                                    ALU.is_equal).then_inc(b_oh, 1)
            dve.wait_ge(b_sce, 1)
            step(ts(mv[:, 5, :], mv[:, 5, :], 1.0, None, ALU.add))
            step(nc.vector.reciprocal(mv[:, 5, :], mv[:, 5, :]))
            dve.wait_ge(b_cnt, 1)
            step(nc.vector.tensor_copy(rt[:, 2, :], ps[6][:, 256:512]))
            for e in range(E):
                step(nc.vector.tensor_tensor_scan(v3(3)[:, :, e], ones[:, 0:T], v3(2)[:, :, e], 0.0, ALU.mult, ALU.add))
            step(nc.vector.tensor_copy(cnt[:, 0, :], v3(3)[:, T - 1, :]))
            step(ts(cnt[:, 1, :], cnt[:, 0, :], float(P - 1), None, ALU.add))
            step(nc.vector.tensor_copy(cnti[:, :], cnt[:, 1, :]))
            step(ts(cnti[:, :], cnti[:, :], 7, None, ALU.arith_shift_right))
            step(nc.vector.tensor_copy(cnt[:, 2, :], cnti[:, :]))
            step(nc.vector.tensor_tensor_scan(cnt[:, 3, :], ones[:, 0:E], cnt[:, 2, :], 0.0, ALU.mult, ALU.add))
            step(tt(cnt[:, 4, :], cnt[:, 3, :], cnt[:, 2, :], ALU.subtract))
            step(ts(cnt[:, 4, :], cnt[:, 4, :], float(P), None, ALU.mult))
            step(tt(rt[:, 3, :], rt[:, 3, :], rt[:, 2, :], ALU.subtract))
            step(tt(rt[:, 3, :], rt[:, 3, :], ps[6][:, 0:256], ALU.add))
            step(tt(v3(3), v3(3), cnt[:, 4, :].unsqueeze(1).broadcast_to([P, T, E]), ALU.add))
            step(tt(rt[:, 3, :], rt[:, 3, :], rt[:, 1, :], ALU.mult))
            step(nc.vector.tensor_reduce(mv[:, 3, :], v3(3), AX, ALU.add))
            step(nc.vector.tensor_copy(slot[:, :], mv[:, 3, :]))
            step(tt(etab[:, :, :], cst[:, C_TILE:C_TILE + NT].unsqueeze(2).broadcast_to([P, NT, E]),
                    cnt[:, 3, :].unsqueeze(1).broadcast_to([P, NT, E]), ALU.is_ge))
            step(nc.vector.tensor_reduce(etabs[:, :], etab[:, :, :], AX, ALU.add))
            step(ts(etabs[:, :], etabs[:, :], float(E - 1), float(WEXP), ALU.min, ALU.mult))
            nc.vector.tensor_copy(etabi[:, :], etabs[:, :]).then_inc(b_tab, 1)
            base_b = base_a + BB * T + at[0]

            dve.wait_ge(s_fill, 16 * (NT // 4))

            def send(q, k, sent):
                t = q * 4
                if sent:
                    dve.wait_ge(b_scat[k], q * 16)
                nc.vector.tensor_copy(idx[:, k:k + 1], slot[:, bass.ds(t + k, 1)])
                ts(stage[:, k:k + 1, :], X[:, bass.ds(t + k, 1), :], mv[:, 5, bass.ds(t + k, 1)], None,
                   ALU.mult).then_inc(b_row, 1)
            for k in range(4):
                send(0, k, False)
            with dve.Fori(1, T // 4) as q:
                for k in range(4):
                    send(q, k, True)

            def b_tile(i, u):
                step, _ = chain(i * BB + base_b)
                swiglu(i, u, step, ps[2 + u], b_gu, b_exp, b_h, b_hTp)
            by_tile(dve, NT, b_tile)
            base_c = base_b + BB * NT

            dve.wait_ge(b_halo, 16 * 8)
            dve.wait_ge(b_dn, NT)

            S0 = POOL_J
            SJ = NJ - POOL_J

            def keys(r, u):
                wait_turn(dve, c_q[u], r)
                tt(prodA[u][:, S0:NJ, :], K[:, bass.ds(r + S0, SJ), :],
                   xnb[:, u, :].unsqueeze(1).broadcast_to([P, SJ, C]), ALU.mult).then_inc(c_pa, 1)

            def scores(r, u, step, edge):
                dve.wait_ge(c_pa, 2 * r + 2)
                if not (static(r) and r < 2):
                    dve.wait_ge(c_pb, r - 1)
                s = small[:, u, :]
                s3 = s.rearrange("p (j h) -> p j h", h=H)
                for_j = s.rearrange("p (j h) -> p h j", h=H)
                i = nc.vector.tensor_reduce(s3, prodA[u].rearrange("p j (h d) -> p j h d", d=HD), AX, ALU.add)
                i.then_inc(c_red, 1)
                dve.wait_ge(c_red, r + 1)
                step(tt(s, s, wj, ALU.mult))
                if edge:
                    lo, n = (0, HALO_L - r) if r < HALO_L else (T + HALO_L - r, NJ - (T + HALO_L - r))
                    m = C_EDGE + (0 if r < HALO_L else 1)
                    step(ts(s[:, lo * H:(lo + n) * H], s[:, lo * H:(lo + n) * H], cst[:, m:m + 1], None, ALU.add))
                step(nc.vector.tensor_reduce(mx[:, 0, :], for_j, AX, ALU.max))
                tt(s3, s3, mx[:, 0, :].unsqueeze(1).broadcast_to([P, NJ, H]), ALU.subtract).then_inc(c_s, 1)

            def values(r, u, step):
                dve.wait_ge(c_e, r + 1)
                if not (static(r) and r < 1):
                    dve.wait_ge(c_sum, r)
                tt(prodB[:, S0:NJ, :].rearrange("p j (h d) -> p j h d", d=HD),
                   V[:, bass.ds(r + S0, SJ), :].rearrange("p j (h d) -> p j h d", d=HD),
                   small[:, u, S0 * H:].rearrange("p (j h) -> p j h", h=H).unsqueeze(3)
                   .broadcast_to([P, SJ, H, HD]), ALU.mult).then_inc(c_pbd, 1)
                step(nc.vector.tensor_reduce(mx[:, 1, :], small[:, u, :].rearrange("p (j h) -> p h j", h=H), AX, ALU.add))
                step(nc.vector.reciprocal(mx[:, 1, :], mx[:, 1, :]))

            def expert_sum(r, u):
                wait_turn(dve, c_g[u], r)
                if static(r):
                    dve.wait_ge(c_ld[u], 32 * (r // 2 + 1))
                    if r >= 2:
                        dve.wait_ge(c_st[u], 16 * (r // 2))
                else:
                    dve.wait_ge(c_ld[u], (r // 2) * 32 + 32)
                    dve.wait_ge(c_st[u], (r // 2) * 16)
                tt(gr[:, u, :], tin[:, u, 1, :], tin[:, u, 2, :], ALU.add).then_inc(c_f, 1)

            def idx_for(r, u):
                if not (static(r) and r < 2):
                    wait_before(dve, c_g[u], r)
                    dve.wait_ge(c_f, r - 1)
                nc.vector.tensor_copy(idx[:, u:u + 1], slot[:, bass.ds(r, 1)]).then_inc(c_idx, 1)

            def attend(r, u):
                dve.wait_ge(c_sum, r + 1)
                if not (static(r) and r < 2):
                    dve.wait_ge(c_oTp, r - 1)
                tt(hb[:, u, :].rearrange("p (h d) -> p h d", d=HD),
                   ps[u][:, 0:C].rearrange("p (h d) -> p h d", d=HD),
                   mx[:, 1, :].unsqueeze(2).broadcast_to([P, H, HD]), ALU.mult).then_inc(c_on, 1)

            def finish(r, u, step):
                dve.wait_ge(c_fe, r + 1)
                step(ts(ga[:, u, :], ga[:, u, :], 1.0, None, ALU.add))
                step(nc.vector.reciprocal(ga[:, u, :], ga[:, u, :]))
                step(tt(ga[:, u, :], ga[:, u, :], gr[:, u, :], ALU.mult))
                dve.wait_ge(c_pr, r + 1)
                step(tt(gr[:, u, :], ps[3][:, 0:C], pbias[:, :], ALU.add))
                step(tt(gr[:, u, :], gr[:, u, :], ga[:, u, :], ALU.mult))
                tt(gr[:, u, :], gr[:, u, :], tin[:, u, 0, :], ALU.add).then_inc(c_out, 1)

            counts = [base_c]

            def tile(r, u, edge_next=False):
                k0 = counts[0] if static(r) else None
                base = k0 if static(r) else r * PER + loop_base[0]
                step, at = chain(base)
                idx_for(r, u)
                if not (static(r) and r == T - 1):
                    keys(r + 1, 1 - u)
                expert_sum(r, u)
                values(r, u, step)
                if not (static(r) and r == 0):
                    finish(r - 1, 1 - u, step)
                if not (static(r) and r == T - 1):
                    scores(r + 1, 1 - u, step, edge_next)
                attend(r, u)
                return at[0]
            PER = 2 + 5 + 2
            loop_base = [0]
            keys(0, 0)
            step, at = chain(counts[0])
            scores(0, 0, step, True)
            counts[0] += at[0]
            FIRST, LAST = HALO_L, T - HALO_R + 1
            for r in range(FIRST):
                counts[0] += tile(r, r % 2, r + 1 < FIRST)
            loop_base[0] = counts[0] - PER * FIRST
            with dve.Fori(FIRST // 2, (LAST - 2) // 2) as pair:
                assert tile(pair * 2, 0) == PER
                assert tile(pair * 2 + 1, 1) == PER
            counts[0] += PER * (LAST - 2 - FIRST)
            for r in range(LAST - 2, T):
                counts[0] += tile(r, r % 2, T - HALO_R < r + 1 < T)
            step, at = chain(counts[0])
            finish(T - 1, 1, step)

        @block.tensor
        def _(pe):
            mm = nc.tensor.matmul
            pe.wait_ge(s_const, 16)
            pe.wait_ge(s_raw, 32)
            for b in range(4):
                for k in range(4):
                    kc, a = b // 2, 4 * (b % 2) + k
                    last = nc.tensor.transpose(ps[b][:, k * P:(k + 1) * P], raw[:, a, kc * P:(kc + 1) * P], ident)
                last.then_inc(s_wtp, 1)
            pe.wait_ge(s_wtc, 4)
            pe.wait_ge(s_w, 16 * 5)

            def flip(dst, src, s):
                for k in range(KC):
                    last = nc.tensor.transpose(dst[:, k * P:(k + 1) * P], src[:, k * P:(k + 1) * P], ident)
                last.then_inc(s, 1)

            def times(dst, lhsT, rhs, s=None):
                for k in range(KC):
                    last = mm(dst, lhsT[:, k * P:(k + 1) * P], rhs(k), start=k == 0, stop=k == KC - 1)
                if s is not None:
                    last.then_inc(s, 1)

            def a_flip(r, u):
                pe.wait_ge(a_xn, r + 1)
                if not (static(r) and r < 2):
                    pe.wait_ge(a_xT, r - 1)
                flip(ps[u], xnb[:, u, :], a_xTp)

            def a_tile(r, u):
                if static(r) and r == 0:
                    a_flip(0, 0)
                if not (static(r) and r == T - 1):
                    a_flip(r + 1, 1 - u)
                pe.wait_ge(a_xT, r + 1)
                if not (static(r) and r < 2):
                    pe.wait_ge(a_kv, r - 1)
                times(ps[2 + u][:, :], xT[:, u, :], lambda k: wt[:, k, 0:512], a_qk)
                if not (static(r) and r == 0):
                    pe.wait_ge(a_kv, r)
                times(ps[4][:, 0:C], xT[:, u, :], lambda k: wt[:, k, 512:768])
                times(ps[4][:, C:C + E], xT[:, u, :], lambda k: wrt[:, k, :], a_vr)
                if not (static(r) and r == 0):
                    pe.wait_ge(a_h, r)
                times(ps[5][:, :], xT[:, u, :], lambda k: wgu[:, k, :], a_gu)
                if not (static(r) and r == 0):
                    a_down(r - 1, 1 - u)

            def a_down(r, u):
                pe.wait_ge(a_h, r + 1)
                if not (static(r) and r == 0):
                    pe.wait_ge(a_hT, r)
                flip(ps[6], hb[:, u, :], a_hTp)
                pe.wait_ge(a_hT, r + 1)
                if not (static(r) and r == 0):
                    pe.wait_ge(a_sh, r)
                times(ps[7][:, 0:C], hT[:, u, :], lambda k: wdn[:, k, :], a_dn)
            by_tile(pe, T, a_tile)
            a_down(T - 1, 1)

            pe.wait_ge(b_oh, 1)
            pe.wait_ge(a_hT, T)
            mm(ps[6][:, 0:256], tri, rt[:, 1, :], start=True, stop=True)
            mm(ps[6][:, 256:512], ones, rt[:, 1, :], start=True, stop=True).then_inc(b_cnt, 1)
            pe.wait_ge(b_tab, 1)
            pe.wait_ge(b_w0, 16 * 3 * E0)
            pe.wait_ge(b_w1, 16 * 3 * (E - E0))

            def b_flip(i, u):
                wait_turn(pe, b_in[u], i)
                if not (static(i) and i < 2):
                    pe.wait_ge(b_xT, i - 1)
                flip(ps[u], xnb[:, u, :], b_xTp)

            def offset(i):
                return pe.value_load(etabi[0:1, bass.ds(i, 1)], min_val=0, max_val=(E - 1) * WEXP)

            def b_tile(i, u):
                if static(i) and i == 0:
                    b_flip(0, 0)
                if not (static(i) and i == NT - 1):
                    b_flip(i + 1, 1 - u)
                o = offset(i)
                pe.wait_ge(b_xT, i + 1)
                if not (static(i) and i < 2):
                    pe.wait_ge(b_h, i - 1)
                times(ps[2 + u][:, :], xT[:, u, :], lambda k: R[:, bass.ds(o + k * 2 * F, 2 * F)], b_gu)
                if not (static(i) and i == 0):
                    b_down(i - 1, 1 - u)

            def b_down(i, u):
                o = offset(i)
                pe.wait_ge(b_h, i + 1)
                if not (static(i) and i < 2):
                    pe.wait_ge(b_hT, i - 1)
                flip(ps[4 + u], hb[:, u, :], b_hTp)
                pe.wait_ge(b_hT, i + 1)
                if not (static(i) and i < 2):
                    pe.wait_ge(b_y, i - 1)
                times(ps[6 + u][:, 0:C], hT[:, u, :], lambda k: R[:, bass.ds(o + KC * 2 * F + k * C, C)], b_dn)
            by_tile(pe, NT, b_tile)
            b_down(NT - 1, 1)

            def c_tile(r, u):
                pe.wait_ge(c_pbd, r + 1)
                pe.wait_ge(c_pb, r + 1)
                if not (static(r) and r < 2):
                    pe.wait_ge(c_on, r - 1)
                for j in range(NJ):
                    last = mm(ps[u][:, 0:C], ident, prodB[:, j, :], start=j == 0, stop=j == NJ - 1)
                last.then_inc(c_sum, 1)
                c_proj(r, u)

            def c_proj(r, u):
                pe.wait_ge(c_on, r + 1)
                if not (static(r) and r == 0):
                    pe.wait_ge(c_oT, r)
                flip(ps[2], hb[:, u, :], c_oTp)
                pe.wait_ge(c_oT, r + 1)
                if not (static(r) and r == 0):
                    pe.wait_ge(c_out, r)
                times(ps[3][:, 0:C], hT[:, u, :], lambda k: wt[:, k, 768:1024], c_pr)
            by_tile(pe, T, c_tile)


_INS = ["L0_attn_x", "L0_attn_qkv_w", "L0_attn_proj_w", "L0_attn_proj_b", "L0_ffn_router_w", "L0_ffn_gate_w",
        "L0_ffn_up_w", "L0_ffn_down_w", "L0_ffn_shared_gate_w", "L0_ffn_shared_up_w", "L0_ffn_shared_down_w"]


def kernel(**inputs):
    import numpy as _np
    import concourse.bacc as _bacc
    from concourse.bass_utils import run_bass_kernel_spmd as _run

    nc = _bacc.Bacc("TRN2", target_bir_lowering=False, num_devices=1)
    arrays, args = {}, []
    for name in _INS:
        a = _np.ascontiguousarray(inputs[name])
        if name == "L0_attn_x":
            a = a.reshape(BATCH * SEQ, C)
        arrays["in_" + name] = a
        args.append(nc.dram_tensor("in_" + name, a.shape, F32, kind="ExternalInput").ap())
    arrays["const"] = constants()
    args.append(nc.dram_tensor("const", (P, C_END), F32, kind="ExternalInput").ap())
    args.append(nc.dram_tensor("out_0", (BATCH * SEQ, C), F32, kind="ExternalOutput").ap())
    for name, shape in (("q_dram", (P, T, C)), ("shared_dram", (P, T, C)), ("xs_dram", (NT * P, C)), ("ys_dram", (NT * P, C))):
        args.append(nc.dram_tensor(name, shape, F32, kind="Internal").ap())
    build(nc, *args)
    r = _run(nc, [arrays], core_ids=[0])
    return r.results[0]["out_0"].reshape(BATCH, SEQ, C)
```

```python
from contextlib import ExitStack

import numpy as np

import concourse.bass as bass
from concourse import mybir

F32 = mybir.dt.float32
I32 = mybir.dt.int32
U32 = mybir.dt.uint32
ALU = mybir.AluOpType
ACT = mybir.ActivationFunctionType
AX = mybir.AxisListType.X

P = 128
BATCH, SEQ, C = 8, 512, 256
H, HD = 32, 8
WIN = 8
NJ = 2 * WIN
E, F = 8, 256
T = BATCH * SEQ // P
SEGS = SEQ // T
KC = C // P
HALO_L, HALO_R = WIN, WIN - 1
NPOS = T + HALO_L + HALO_R
NT = T + E
EPS = 1e-5
NEG = -3e38
WEXP = KC * 2 * F + KC * C
POOL_J = 12

C_ID, C_TRI, C_ONE = 0, P, 2 * P
C_WJ = 3 * P
C_EDGE = C_WJ + NJ * H
C_FIRST = C_EDGE + 4 * WIN
C_TILE = C_FIRST + E
C_END = C_TILE + NT


def constants():
    c = np.zeros((P, C_END), np.float32)
    c[:, C_ID:C_ID + P] = np.eye(P)
    c[:, C_TRI:C_TRI + P] = np.triu(np.ones((P, P)), 1)
    c[:, C_ONE:C_ONE + P] = 1.0
    d = np.abs(np.arange(NJ) - WIN).astype(np.float32)
    c[:, C_WJ:C_WJ + NJ * H] = np.repeat((WIN - d / 2.0) / WIN * np.float32(HD ** -0.5), H)
    p = np.arange(P)
    c[:, C_EDGE:C_EDGE + WIN] = np.where(p % SEGS == 0, NEG, 0.0)[:, None]
    c[:, C_EDGE + 3 * WIN:C_EDGE + 4 * WIN] = np.where(p % SEGS == SEGS - 1, NEG, 0.0)[:, None]
    c[:, C_FIRST:C_FIRST + E] = E - np.arange(E)
    c[:, C_TILE:C_TILE + NT] = np.arange(NT)
    return c


def static(t):
    return isinstance(t, int)


def by_tile(eng, n, body, period=2):
    for t in range(period):
        body(t, t)
    with eng.Fori(1, n // period - 1) as turn:
        for k in range(period):
            body(turn * period + k, k)
    for t in range(n - period, n):
        body(t, t % period)


def wait_turn(eng, sem, t, period=2):
    eng.wait_ge(sem, (t // period) * 16 + 16)


def wait_before(eng, sem, t, period=2):
    eng.wait_ge(sem, (t // period) * 16)


def build(nc, x, qkv_w, proj_w, proj_b, router_w, gate_w, up_w, down_w, sgate_w, sup_w, sdown_w,
          const, out, q_dram, shared_dram, gate_dram, xs_dram, ys_dram):
    ctx = ExitStack()
    with ctx:
        def sb(name, shape, dt=F32):
            return ctx.enter_context(nc.sbuf_tensor(name, shape, dt))

        def sem(name):
            return ctx.enter_context(nc.semaphore(name))

        K = sb("K", [P, NPOS, C])
        V = sb("V", [P, NPOS, C])
        R = sb("R", [P, E * WEXP])
        cst = sb("cst", [P, C_END])
        wt = sb("wt", [P, KC, 4 * C])
        U = sb("U", [P, 4160])
        wgu = U[:, 0:1024].rearrange("p (k f) -> p k f", k=KC)
        wdn = U[:, 1024:1536].rearrange("p (k c) -> p k c", k=KC)
        stage = U[:, 1536:2560].rearrange("p (k c) -> p k c", k=4)
        rt = U[:, 2560:3584].rearrange("p (k c) -> p k c", k=4)
        lg = U[:, 3584:3840].rearrange("p (t e) -> p t e", e=E)
        etab = U[:, 3840:3840 + NT * E].rearrange("p (t e) -> p t e", e=E)
        wrt = sb("wrt", [P, KC, E])
        pbias = sb("pbias", [P, C])
        xnb = sb("xnb", [P, 2, C])
        xT = sb("xT", [P, 2, C])
        hb = sb("hb", [P, 2, C])
        hT = sb("hT", [P, 2, C])
        ga = sb("ga", [P, 2, C])
        gr = sb("gr", [P, 2, C])
        tin = sb("tin", [P, 2, 2, C])
        small = sb("small", [P, 2, NJ * H])
        mx = sb("mx", [P, 3, H])
        stats = sb("stats", [P, T, 6])
        mv = sb("mv", [P, 8, T])
        cnt = sb("cnt", [P, 8, E])
        cnti = sb("cnti", [P, E], I32)
        slot = sb("slot", [P, T], U32)
        etabs = sb("etabs", [P, NT])
        etabi = sb("etabi", [P, NT], I32)

        ident = cst[:, C_ID:C_ID + P]
        tri = cst[:, C_TRI:C_TRI + P]
        ones = cst[:, C_ONE:C_ONE + P]
        wj = cst[:, C_WJ:C_WJ + NJ * H]
        XO = 4096
        X = R[:, XO:XO + T * C].rearrange("p (t c) -> p t c", c=C)
        raw = K[:, 0:8, :]
        prodA = [R[:, i * NJ * C:(i + 1) * NJ * C].rearrange("p (j c) -> p j c", c=C) for i in range(2)]
        prodB = [x_.rearrange("p (j c) -> p j c", c=C) for x_ in (R[:, 2 * NJ * C:3 * NJ * C], U[:, 0:NJ * C])]
        GT = 4
        grow = R[:, 0:T * C]
        gsh = R[:, T * C:T * C + 4 * GT * C].rearrange("p (k c) -> p k c", k=4)

        ps = [ctx.enter_context(nc.psum_tensor(f"ps{i}", [P, 512], F32)) for i in range(8)]

        s_const, s_raw, s_w, s_zero, s_fill = (sem(n) for n in ("s_const", "s_raw", "s_w", "s_zero", "s_fill"))
        s_x = [sem(f"s_x{i}") for i in range(4)]
        s_wtp, s_wtc = sem("s_wtp"), sem("s_wtc")
        s_dve = sem("s_dve")
        s_bn = sem("s_bn")
        s_var, s_sqrt = sem("s_var"), sem("s_sqrt")
        a_xn, a_xTp, a_xT, a_qk, a_vr, a_gu = (sem("a_" + n) for n in ("xn", "xTp", "xT", "qk", "vr", "gu"))
        a_exp, a_h, a_hTp, a_hT, a_dn, a_lg = (sem("a_" + n) for n in ("exp", "h", "hTp", "hT", "dn", "lg"))
        a_q, a_kv, a_sh = (sem("a_" + n) for n in ("q", "kv", "sh"))
        a_qst, a_sst = ([sem(f"a_{n}{i}") for i in range(2)] for n in ("qst", "sst"))
        b_oh, b_cnt, b_sc, b_sce, b_tab, b_row, b_halo, b_w = (
            sem("b_" + n) for n in ("oh", "cnt", "sc", "sce", "tab", "row", "halo", "w"))
        SENDS = 4
        b_scat = [sem(f"b_scat{i}") for i in range(SENDS)]
        b_in = [sem(f"b_in{i}") for i in range(4)]
        b_st = [sem(f"b_st{i}") for i in range(2)]
        b_xTp, b_xT, b_gu, b_exp, b_h, b_hTp, b_hT, b_dn, b_y = (
            sem("b_" + n) for n in ("xTp", "xT", "gu", "exp", "h", "hTp", "hT", "dn", "y"))
        g_rows = [sem(f"g_rows{i}") for i in range(T // GT)]
        g_sh = [sem(f"g_sh{i}") for i in range(4)]
        g_f, g_sig, g_g, g_st = (sem("g_" + n) for n in ("f", "sig", "g", "st"))
        c_ld, c_q, c_st = ([sem(f"c_{n}{i}") for i in range(2)] for n in ("ld", "q", "st"))
        c_kp, c_kd, c_vp, c_vd, c_red, c_s, c_e, c_sum, c_on, c_oTp, c_oT, c_pr, c_out = (
            sem("c_" + n) for n in ("kp", "kd", "vp", "vd", "red", "s", "e", "sum", "on", "oTp", "oT", "pr", "out"))

        wexp = R[:, :].rearrange("p (e w) -> p e w", w=WEXP)

        def load_expert(eng, e):
            g = wexp[:, e, 0:KC * 2 * F].rearrange("p (k f) -> p k f", k=KC)
            for w, c0 in ((gate_w, 0), (up_w, F)):
                eng.dma_start(g[:, :, c0:c0 + F], w[e].rearrange("(k p) f -> p k f", p=P)).then_inc(b_w, 16)
            eng.dma_start(wexp[:, e, KC * 2 * F:WEXP].rearrange("p (k c) -> p k c", k=KC),
                          down_w[e].rearrange("(k p) c -> p k c", p=P)).then_inc(b_w, 16)

        E0 = XO // WEXP
        x_v = x.rearrange("(p t) c -> p t c", t=T)
        out_v = out.rearrange("(p t) c -> p t c", t=T)
        XCH = 4
        BB = 1
        block = ctx.enter_context(nc.Block())

        @block.sync
        def _(sp):
            sp.dma_start(cst[:, :], const).then_inc(s_const, 16)
            n = T // XCH
            for i in range(XCH):
                sp.dma_start(X[:, i * n:(i + 1) * n, :], x_v[:, i * n:(i + 1) * n, :]).then_inc(s_x[i], 16)
            sp.dma_start(raw[:, 0:6, :], qkv_w.rearrange("(a p) c -> p a c", p=P)).then_inc(s_raw, 16)
            sp.dma_start(raw[:, 6:8, :], proj_w.rearrange("(a p) c -> p a c", p=P)).then_inc(s_raw, 16)
            for dst, src in ((wgu[:, :, 0:F], sgate_w), (wgu[:, :, F:2 * F], sup_w), (wdn[:, :, :], sdown_w),
                             (wrt[:, :, :], router_w)):
                sp.dma_start(dst, src.rearrange("(k p) f -> p k f", p=P)).then_inc(s_w, 16)
            sp.dma_start(pbias[:, :], proj_b.unsqueeze(0).broadcast_to([P, C])).then_inc(s_w, 16)
            for e in range(E0):
                load_expert(sp, e)
            sp.wait_ge(s_zero, 1)
            for i in range(NT // 4):
                sp.dma_start(xs_dram[i * 4 * P:(i + 1) * 4 * P, :].rearrange("(p r) c -> p r c", r=4),
                             stage[:, :, :]).then_inc(s_fill, 16)

            def save(r, u):
                sp.wait_ge(a_q, r + 1)
                sp.dma_start(q_dram[:, bass.ds(r, 1), :], small[:, u:u + 1, 0:C]).then_inc(a_qst[u], 16)
                if not (static(r) and r < 2):
                    save_shared(r - 2, u)

            def save_shared(r, u):
                sp.wait_ge(a_sh, r + 1)
                sp.dma_start(shared_dram[:, bass.ds(r, 1), :], tin[:, u, 0:1, :]).then_inc(a_sst[u], 16)
            by_tile(sp, T, save)
            save_shared(T - 2, 0)
            save_shared(T - 1, 1)

            for e in range(E0, E):
                tiles = -(-((e + 1) * WEXP - XO) // C)
                n = -(-tiles // (T // SENDS))
                for q in range(n):
                    sp.wait_ge(b_scat[q], 16 * (T // SENDS))
                load_expert(sp, e)

            sp.wait_ge(a_kv, T)
            for t in (K, V):
                sp.dma_start(t[1:P, 0:HALO_L, :], t[0:P - 1, T:T + HALO_L, :]).then_inc(b_halo, 16)
                sp.dma_start(t[0:1, 0:HALO_L, :], t[0:1, T:T + HALO_L, :]).then_inc(b_halo, 16)
                sp.dma_start(t[0:P - 1, HALO_L + T:NPOS, :], t[1:P, HALO_L:HALO_L + HALO_R, :]).then_inc(b_halo, 16)
                sp.dma_start(t[P - 1:P, HALO_L + T:NPOS, :], t[P - 1:P, HALO_L:HALO_L + HALO_R, :]).then_inc(b_halo, 16)

            def rows(i, k):
                if not (static(i) and i < 4):
                    sp.wait_ge(b_xTp, i - 3)
                sp.dma_start(stage[:, k, :], xs_dram[bass.ds(i * P, P), :]).then_inc(b_in[k], 16)
            by_tile(sp, NT, rows, 4)

            def save_gates(c):
                sp.wait_ge(g_g, c + 1)
                sp.dma_start(gate_dram[:, c * GT:(c + 1) * GT, :],
                             grow[:, c * GT * C:(c + 1) * GT * C].rearrange("p (t c) -> p t c", t=GT)).then_inc(g_st, 16)
            for u in range(2):
                sp.wait_ge(a_sst[u], 8 * T)
            sp.wait_ge(b_dn, NT)
            for c in range(T // GT):
                if c >= 4:
                    sp.wait_ge(g_g, c - 3)
                sp.dma_start(gsh[:, c % 4, :].rearrange("p (t c) -> p t c", t=GT),
                             shared_dram[:, c * GT:(c + 1) * GT, :]).then_inc(g_sh[c % 4], 16)
                if c >= 2:
                    save_gates(c - 2)
            save_gates(T // GT - 2)
            save_gates(T // GT - 1)
            sp.wait_ge(g_st, 16 * (T // GT))
            for u in range(2):
                sp.wait_ge(a_qst[u], 8 * T)
                sp.wait_ge(b_st[u], 8 * NT)

            def load_q(r, u):
                if not (static(r) and r < 2):
                    sp.wait_ge(c_kd, r - 1)
                    sp.wait_ge(c_kp, r - 1)
                sp.dma_start(xnb[:, u:u + 1, :], q_dram[:, bass.ds(r, 1), :]).then_inc(c_q[u], 16)

            def store_out(r, u):
                sp.wait_ge(c_out, r + 1)
                sp.dma_start(out_v[:, bass.ds(r, 1), :], gr[:, u:u + 1, :]).then_inc(c_st[u], 16)

            def c_tile(r, u):
                if not (static(r) and r >= T - 2):
                    load_q(r + 2, u)
                if not (static(r) and r < 2):
                    store_out(r - 2, u)
                sp.dma_start(tin[:, u, 0:1, :], x_v[:, bass.ds(r, 1), :]).then_inc(c_ld[u], 16)
                sp.dma_start(tin[:, u, 1:2, :], gate_dram[:, bass.ds(r, 1), :]).then_inc(c_ld[u], 16)
            load_q(0, 0)
            load_q(1, 1)
            by_tile(sp, T, c_tile)
            store_out(T - 2, 0)
            store_out(T - 1, 1)
            for u in range(2):
                sp.wait_ge(c_st[u], 8 * T)

        @block.gpsimd
        def _(pool):
            nc.gpsimd.memset(stage[:, :, :], 0.0).then_inc(s_zero, 1)
            pool.wait_ge(s_fill, 16 * (NT // 4))
            for t in range(T):
                pool.wait_ge(b_row, t // (T // SENDS) + 1)
                pool.indirect_dma_start(xs_dram, bass.IndirectOffsetOnAxis(ap=slot[:, t:t + 1], axis=0),
                                        X[:, t, :], None).then_inc(b_scat[t // (T // SENDS)], 16)
            for u in range(2):
                pool.wait_ge(b_st[u], 8 * NT)
            for t in range(T):
                pool.indirect_dma_start(grow[:, t * C:(t + 1) * C], None, ys_dram,
                                        bass.IndirectOffsetOnAxis(ap=slot[:, t:t + 1], axis=0)).then_inc(g_rows[t // GT], 16)
            pool.wait_ge(b_halo, 16 * 8)
            pool.wait_ge(g_st, 16 * (T // GT))
            pool.wait_ge(g_g, T // GT)

            def keys(r, u):
                wait_turn(pool, c_q[u], r)
                if not (static(r) and r < 2):
                    pool.wait_ge(c_red, r - 1)
                nc.gpsimd.tensor_tensor(
                    prodA[u][:, 0:POOL_J, :], K[:, bass.ds(r, POOL_J), :],
                    xnb[:, u, :].unsqueeze(1).broadcast_to([P, POOL_J, C]), ALU.mult).then_inc(c_kp, 1)

            def values(r, u):
                pool.wait_ge(c_e, r + 1)
                if not (static(r) and r < 2):
                    pool.wait_ge(c_sum, r - 1)
                nc.gpsimd.tensor_tensor(
                    prodB[u][:, 0:POOL_J, :].rearrange("p j (h d) -> p j h d", d=HD),
                    V[:, bass.ds(r, POOL_J), :].rearrange("p j (h d) -> p j h d", d=HD),
                    small[:, u, 0:POOL_J * H].rearrange("p (j h) -> p j h", h=H).unsqueeze(3)
                    .broadcast_to([P, POOL_J, H, HD]), ALU.mult).then_inc(c_vp, 1)

            def c_tile(r, u):
                values(r, u)
                if not (static(r) and r >= T - 2):
                    keys(r + 2, u)
            keys(0, 0)
            keys(1, 1)
            by_tile(pool, T, c_tile)

        @block.scalar
        def _(act):
            act.wait_ge(s_var, 1)
            nc.scalar.activation(mv[:, 2, :], mv[:, 1, :], ACT.Sqrt).then_inc(s_sqrt, 1)
            for b in range(4):
                act.wait_ge(s_wtp, b + 1)
                nc.scalar.activation(wt[:, b // 2, 512 * (b % 2):512 * (b % 2) + 512], ps[b][:, :],
                                     ACT.Copy).then_inc(s_wtc, 1)

            def xcopy(r, u):
                act.wait_ge(a_xTp, r + 1)
                if not (static(r) and r < 2):
                    act.wait_ge(a_gu, r - 1)
                nc.scalar.activation(xT[:, u, :], ps[u][:, 0:C], ACT.Copy).then_inc(a_xT, 1)

            def a_tile(r, u):
                if static(r) and r == 0:
                    xcopy(0, 0)
                if not (static(r) and r == T - 1):
                    xcopy(r + 1, 1 - u)
                act.wait_ge(a_qk, r + 1)
                if not (static(r) and r < 2):
                    wait_before(act, a_qst[u], r)
                nc.scalar.activation(small[:, u, 0:C], ps[2 + u][:, 0:C], ACT.Copy).then_inc(a_q, 1)
                nc.scalar.activation(K[:, bass.ds(r + HALO_L, 1), :], ps[2 + u][:, C:2 * C].unsqueeze(1), ACT.Copy)
                act.wait_ge(a_vr, r + 1)
                act.wait_ge(a_lg, r + 1)
                nc.scalar.activation(V[:, bass.ds(r + HALO_L, 1), :], ps[4][:, 0:C].unsqueeze(1), ACT.Copy).then_inc(a_kv, 1)
                act.wait_ge(a_gu, r + 1)
                if not (static(r) and r < 2):
                    act.wait_ge(a_h, r - 1)
                nc.scalar.activation(ga[:, u, :], ps[5][:, 0:F], ACT.Sigmoid).then_inc(a_exp, 1)
                if not (static(r) and r < 1):
                    a_hcopy(r - 1, 1 - u)
                if not (static(r) and r < 2):
                    a_down(r - 2, u)

            def a_hcopy(r, u):
                act.wait_ge(a_hTp, r + 1)
                if not (static(r) and r < 2):
                    act.wait_ge(a_dn, r - 1)
                nc.scalar.activation(hT[:, u, :], ps[6][:, 0:F], ACT.Copy).then_inc(a_hT, 1)

            def a_down(r, u):
                act.wait_ge(a_dn, r + 1)
                if not (static(r) and r < 2):
                    wait_before(act, a_sst[u], r)
                nc.scalar.activation(tin[:, u, 0, :], ps[7][:, 0:C], ACT.Copy).then_inc(a_sh, 1)
            by_tile(act, T, a_tile)
            a_down(T - 2, 0)
            a_hcopy(T - 1, 1)
            a_down(T - 1, 1)

            act.wait_ge(b_sc, 1)
            nc.scalar.activation(mv[:, 5, :], mv[:, 4, :], ACT.Sigmoid).then_inc(b_sce, 1)
            for u in range(2):
                act.wait_ge(a_sst[u], 8 * T)

            def b_xcopy(i, u):
                act.wait_ge(b_xTp, i + 1)
                if not (static(i) and i < 2):
                    act.wait_ge(b_gu, i - 1)
                nc.scalar.activation(xT[:, u, :], ps[u][:, 0:C], ACT.Copy).then_inc(b_xT, 1)

            def b_tile(i, k):
                u = k % 2
                if static(i) and i == 0:
                    b_xcopy(0, 0)
                if not (static(i) and i == NT - 1):
                    b_xcopy(i + 1, 1 - u)
                act.wait_ge(b_gu, i + 1)
                if not (static(i) and i < 2):
                    act.wait_ge(b_h, i - 1)
                nc.scalar.activation(ga[:, u, :], ps[2 + u][:, 0:F], ACT.Sigmoid).then_inc(b_exp, 1)
                if not (static(i) and i < 1):
                    b_hcopy(i - 1, 1 - u)
                if not (static(i) and i < 2):
                    b_down(i - 2, u)

            def b_hcopy(i, u):
                act.wait_ge(b_hTp, i + 1)
                if not (static(i) and i < 2):
                    act.wait_ge(b_dn, i - 1)
                nc.scalar.activation(hT[:, u, :], ps[4 + u][:, 0:F], ACT.Copy).then_inc(b_hT, 1)

            def b_down(i, u):
                act.wait_ge(b_dn, i + 1)
                if not (static(i) and i < 2):
                    wait_before(act, b_st[u], i)
                nc.scalar.activation(tin[:, u, 0, :], ps[6 + u][:, 0:C], ACT.Copy).then_inc(b_y, 1)
                act.wait_ge(b_y, i + 1)
                act.dma_start(ys_dram[bass.ds(i * P, P), :], tin[:, u, 0, :]).then_inc(b_st[u], 16)
            by_tile(act, NT, b_tile)
            b_down(NT - 2, 0)
            b_hcopy(NT - 1, 1)
            b_down(NT - 1, 1)

            for c in range(T // GT):
                act.wait_ge(g_f, c + 1)
                nc.scalar.activation(gsh[:, c % 4, :], grow[:, c * GT * C:(c + 1) * GT * C], ACT.Sigmoid).then_inc(g_sig, 1)

            def c_exp(r, u):
                act.wait_ge(c_s, r + 1)
                nc.scalar.activation(small[:, u, :], small[:, u, :], ACT.Exp).then_inc(c_e, 1)

            def c_ocopy(r, u):
                act.wait_ge(c_oTp, r + 1)
                nc.scalar.activation(hT[:, u, :], ps[2][:, 0:C], ACT.Copy).then_inc(c_oT, 1)

            def c_tile(r, u):
                if not (static(r) and r == T - 1):
                    c_exp(r + 1, 1 - u)
                if not (static(r) and r < 1):
                    c_ocopy(r - 1, 1 - u)
            c_exp(0, 0)
            by_tile(act, T, c_tile)
            c_ocopy(T - 1, 1)

        @block.vector
        def _(dve):
            def chain(base):
                n = [0]

                def step(ins):
                    n[0] += 1
                    ins.then_inc(s_dve, 1)
                    dve.wait_ge(s_dve, base + n[0])
                return step, n
            tt, ts = nc.vector.tensor_tensor, nc.vector.tensor_scalar
            n = T // XCH
            for i in range(XCH):
                dve.wait_ge(s_x[i], 16)
                with dve.Fori(i * n, (i + 1) * n) as t:
                    nc.vector.bn_stats(stats[:, bass.ds(t, 1), :], X[:, bass.ds(t, 1), :]).then_inc(s_bn, 1)
            dve.wait_ge(s_const, 16)
            dve.wait_ge(s_bn, T)
            step, at = chain(0)
            me, m2e, mo, m2o = (stats[:, :, k] for k in (1, 2, 4, 5))
            step(ts(mv[:, 7, :], me, 0.0, None, ALU.add))
            step(tt(mv[:, 0, :], mv[:, 7, :], mo, ALU.add))
            step(tt(mv[:, 3, :], me, mo, ALU.subtract))
            step(tt(mv[:, 4, :], m2e, m2o, ALU.add))
            step(tt(mv[:, 3, :], mv[:, 3, :], mv[:, 3, :], ALU.mult))
            step(ts(mv[:, 4, :], mv[:, 4, :], 1.0 / C, EPS, ALU.mult, ALU.add))
            step(ts(mv[:, 0, :], mv[:, 0, :], 0.5, None, ALU.mult))
            step(ts(mv[:, 3, :], mv[:, 3, :], 0.25, None, ALU.mult))
            step(tt(mv[:, 1, :], mv[:, 3, :], mv[:, 4, :], ALU.add))
            nc.vector.tensor_copy(mv[:, 7, :], mv[:, 1, :]).then_inc(s_var, 1)
            dve.wait_ge(s_sqrt, 1)
            step(nc.vector.reciprocal(mv[:, 3, :], mv[:, 2, :]))
            step(tt(mv[:, 3, :], mv[:, 3, :], mv[:, 1, :], ALU.mult))
            step(tt(mv[:, 3, :], mv[:, 3, :], mv[:, 2, :], ALU.add))
            step(ts(mv[:, 3, :], mv[:, 3, :], 0.5, None, ALU.mult))
            step(nc.vector.reciprocal(mv[:, 6, :], mv[:, 3, :]))
            base_a = at[0]

            def norm(r, u):
                if not (static(r) and r < 2):
                    dve.wait_ge(a_xTp, r - 1)
                a = (X[:, bass.ds(r, 1), :], mv[:, 0, bass.ds(r, 1)], mv[:, 6, bass.ds(r, 1)], ALU.subtract, ALU.mult)
                ts(xnb[:, u:u + 1, :], *a).then_inc(a_xn, 1)
                ts(X[:, bass.ds(r, 1), :], *a)

            def swiglu(r, u, step, gu, s_gate, s_h, free):
                dve.wait_ge(s_gate, r + 1)
                step(tt(gr[:, u, :], gu[:, 0:F], ga[:, u, :], ALU.mult))
                if not (static(r) and r < 2):
                    dve.wait_ge(free, r - 1)
                tt(hb[:, u, :], gu[:, F:2 * F], gr[:, u, :], ALU.mult).then_inc(s_h, 1)

            def a_tile(r, u):
                if not (static(r) and r >= T - 2):
                    norm(r + 2, u)
                dve.wait_ge(a_vr, r + 1)
                nc.vector.tensor_copy(lg[:, bass.ds(r, 1), :], ps[4][:, C:C + E].unsqueeze(1)).then_inc(a_lg, 1)
                step, _ = chain(r * BB + base_a)
                swiglu(r, u, step, ps[5], a_exp, a_h, a_hTp)
            norm(0, 0)
            norm(1, 1)
            by_tile(dve, T, a_tile)

            step, at = chain(base_a + BB * T)
            dve.wait_ge(a_lg, T)
            v3 = lambda k: rt[:, k, :].rearrange("p (t e) -> p t e", e=E)
            step(nc.vector.tensor_reduce(mv[:, 4, :], lg[:, :, :], AX, ALU.max))
            nc.vector.tensor_copy(mv[:, 7, :], mv[:, 4, :]).then_inc(b_sc, 1)
            step(tt(v3(0), lg[:, :, :], mv[:, 4, :].unsqueeze(2).broadcast_to([P, T, E]), ALU.is_ge))
            first = cst[:, C_FIRST:C_FIRST + E].unsqueeze(1).broadcast_to([P, T, E])
            step(tt(v3(0), v3(0), first, ALU.mult))
            step(nc.vector.tensor_reduce(mv[:, 3, :], v3(0), AX, ALU.max))
            nc.vector.tensor_tensor(v3(1), first, mv[:, 3, :].unsqueeze(2).broadcast_to([P, T, E]),
                                    ALU.is_equal).then_inc(b_oh, 1)
            dve.wait_ge(b_cnt, 1)
            step(nc.vector.tensor_copy(rt[:, 2, :], ps[6][:, 256:512]))
            for e in range(E):
                step(nc.vector.tensor_tensor_scan(v3(3)[:, :, e], ones[:, 0:T], v3(2)[:, :, e], 0.0, ALU.mult, ALU.add))
            step(nc.vector.tensor_copy(cnt[:, 0, :], v3(3)[:, T - 1, :]))
            step(ts(cnt[:, 1, :], cnt[:, 0, :], float(P - 1), None, ALU.add))
            step(nc.vector.tensor_copy(cnti[:, :], cnt[:, 1, :]))
            step(ts(cnti[:, :], cnti[:, :], 7, None, ALU.arith_shift_right))
            step(nc.vector.tensor_copy(cnt[:, 2, :], cnti[:, :]))
            step(nc.vector.tensor_tensor_scan(cnt[:, 3, :], ones[:, 0:E], cnt[:, 2, :], 0.0, ALU.mult, ALU.add))
            step(tt(cnt[:, 4, :], cnt[:, 3, :], cnt[:, 2, :], ALU.subtract))
            step(ts(cnt[:, 4, :], cnt[:, 4, :], float(P), None, ALU.mult))
            step(tt(rt[:, 3, :], rt[:, 3, :], rt[:, 2, :], ALU.subtract))
            step(tt(rt[:, 3, :], rt[:, 3, :], ps[6][:, 0:256], ALU.add))
            step(tt(v3(3), v3(3), cnt[:, 4, :].unsqueeze(1).broadcast_to([P, T, E]), ALU.add))
            step(tt(rt[:, 3, :], rt[:, 3, :], rt[:, 1, :], ALU.mult))
            step(nc.vector.tensor_reduce(mv[:, 3, :], v3(3), AX, ALU.add))
            step(nc.vector.tensor_copy(slot[:, :], mv[:, 3, :]))
            dve.wait_ge(b_sce, 1)
            for q in range(SENDS):
                n = T // SENDS
                tt(X[:, q * n:(q + 1) * n, :], X[:, q * n:(q + 1) * n, :],
                   mv[:, 5, q * n:(q + 1) * n].unsqueeze(2).broadcast_to([P, n, C]), ALU.mult).then_inc(b_row, 1)
            step(tt(etab[:, :, :], cst[:, C_TILE:C_TILE + NT].unsqueeze(2).broadcast_to([P, NT, E]),
                    cnt[:, 3, :].unsqueeze(1).broadcast_to([P, NT, E]), ALU.is_ge))
            step(nc.vector.tensor_reduce(etabs[:, :], etab[:, :, :], AX, ALU.add))
            step(ts(etabs[:, :], etabs[:, :], float(E - 1), float(WEXP), ALU.min, ALU.mult))
            nc.vector.tensor_copy(etabi[:, :], etabs[:, :]).then_inc(b_tab, 1)
            base_b = base_a + BB * T + at[0]

            def b_tile(i, u):
                step, _ = chain(i * BB + base_b)
                swiglu(i, u, step, ps[2 + u], b_exp, b_h, b_hTp)
            by_tile(dve, NT, b_tile)
            base_c = base_b + BB * NT

            for c in range(T // GT):
                mine = grow[:, c * GT * C:(c + 1) * GT * C]
                dve.wait_ge(g_rows[c], 16 * GT)
                dve.wait_ge(g_sh[c % 4], 16 * (c // 4 + 1))
                tt(mine, mine, gsh[:, c % 4, :], ALU.add).then_inc(g_f, 1)
                dve.wait_ge(g_sig, c + 1)
                tt(mine, mine, gsh[:, c % 4, :], ALU.mult).then_inc(g_g, 1)

            dve.wait_ge(b_halo, 16 * 8)
            dve.wait_ge(g_st, 16 * (T // GT))
            S0 = POOL_J
            SJ = NJ - POOL_J

            def keys(r, u):
                wait_turn(dve, c_q[u], r)
                tt(prodA[u][:, S0:NJ, :], K[:, bass.ds(r + S0, SJ), :],
                   xnb[:, u, :].unsqueeze(1).broadcast_to([P, SJ, C]), ALU.mult).then_inc(c_kd, 1)

            def scores(r, u, step, edge):
                dve.wait_ge(c_kp, r + 1)
                dve.wait_ge(c_kd, r + 1)
                if not (static(r) and r < 2):
                    dve.wait_ge(c_vp, r - 1)
                s = small[:, u, :]
                s3 = s.rearrange("p (j h) -> p j h", h=H)
                for_j = s.rearrange("p (j h) -> p h j", h=H)
                nc.vector.tensor_reduce(s3, prodA[u].rearrange("p j (h d) -> p j h d", d=HD), AX, ALU.add).then_inc(c_red, 1)
                dve.wait_ge(c_red, r + 1)
                step(tt(s, s, wj, ALU.mult))
                if edge is not None:
                    at = C_EDGE if edge == "first" else C_EDGE + 2 * WIN + WIN - T
                    half = s3[:, 0:WIN, :] if edge == "first" else s3[:, WIN:NJ, :]
                    step(tt(half, half, cst[:, bass.ds(r + at, WIN)].unsqueeze(2).broadcast_to([P, WIN, H]), ALU.add))
                step(nc.vector.tensor_reduce(mx[:, 0, :], for_j, AX, ALU.max))
                tt(s3, s3, mx[:, 0, :].unsqueeze(1).broadcast_to([P, NJ, H]), ALU.subtract).then_inc(c_s, 1)

            def values(r, u, step):
                dve.wait_ge(c_e, r + 1)
                if not (static(r) and r < 2):
                    dve.wait_ge(c_sum, r - 1)
                tt(prodB[u][:, S0:NJ, :].rearrange("p j (h d) -> p j h d", d=HD),
                   V[:, bass.ds(r + S0, SJ), :].rearrange("p j (h d) -> p j h d", d=HD),
                   small[:, u, S0 * H:].rearrange("p (j h) -> p j h", h=H).unsqueeze(3)
                   .broadcast_to([P, SJ, H, HD]), ALU.mult).then_inc(c_vd, 1)
                if not (static(r) and r < 2):
                    dve.wait_ge(c_on, r - 1)
                step(nc.vector.tensor_reduce(mx[:, 1 + u, :], small[:, u, :].rearrange("p (j h) -> p h j", h=H), AX, ALU.add))
                step(nc.vector.reciprocal(mx[:, 1 + u, :], mx[:, 1 + u, :]))

            def attend(r, u):
                dve.wait_ge(c_sum, r + 1)
                if not (static(r) and r < 2):
                    dve.wait_ge(c_oTp, r - 1)
                tt(hb[:, u, :].rearrange("p (h d) -> p h d", d=HD),
                   ps[u][:, 0:C].rearrange("p (h d) -> p h d", d=HD),
                   mx[:, 1 + u, :].unsqueeze(2).broadcast_to([P, H, HD]), ALU.mult).then_inc(c_on, 1)

            def finish(r, u, step):
                dve.wait_ge(c_pr, r + 1)
                if not (static(r) and r < 2):
                    wait_before(dve, c_st[u], r)
                step(tt(gr[:, u, :], ps[3 + u][:, 0:C], pbias[:, :], ALU.add))
                dve.wait_ge(c_ld[u], (r // 2) * 32 + 32)
                step(tt(gr[:, u, :], gr[:, u, :], tin[:, u, 1, :], ALU.mult))
                tt(gr[:, u, :], gr[:, u, :], tin[:, u, 0, :], ALU.add).then_inc(c_out, 1)

            def c_tile(r, u, step, edge):
                values(r, u, step)
                if not (static(r) and r == T - 1):
                    scores(r + 1, 1 - u, step, edge)
                if not (static(r) and r < 1):
                    attend(r - 1, 1 - u)
                if not (static(r) and r >= T - 2):
                    keys(r + 2, u)
                if not (static(r) and r < 2):
                    finish(r - 2, u, step)

            step, at = chain(base_c)
            keys(0, 0)
            keys(1, 1)
            scores(0, 0, step, "first")
            for r in range(2):
                c_tile(r, r, step, "first")
            steps = base_c + at[0]

            def run(steps, lo, hi, edge):
                per = 6 + (edge is not None)
                with dve.Fori(lo // 2, hi // 2) as pair:
                    for u in range(2):
                        step, at = chain((pair * 2 - lo) * per + (steps + u * per))
                        c_tile(pair * 2 + u, u, step, edge)
                        assert at[0] == per
                return steps + per * (hi - lo)
            steps = run(steps, 2, WIN - 2, "first")
            step, at = chain(steps)
            c_tile(WIN - 2, 0, step, "first")
            c_tile(WIN - 1, 1, step, None)
            steps = run(steps + at[0], WIN, T - WIN, None)
            steps = run(steps, T - WIN, T - 2, "last")
            step, at = chain(steps)
            c_tile(T - 2, 0, step, "last")
            c_tile(T - 1, 1, step, None)
            attend(T - 1, 1)
            finish(T - 2, 0, step)
            finish(T - 1, 1, step)

        @block.tensor
        def _(pe):
            mm = nc.tensor.matmul
            pe.wait_ge(s_const, 16)
            pe.wait_ge(s_raw, 32)
            for b in range(4):
                for k in range(4):
                    kc, a = b // 2, 4 * (b % 2) + k
                    last = nc.tensor.transpose(ps[b][:, k * P:(k + 1) * P], raw[:, a, kc * P:(kc + 1) * P], ident)
                last.then_inc(s_wtp, 1)
            pe.wait_ge(s_wtc, 4)
            pe.wait_ge(s_w, 16 * 5)

            def flip(dst, src, s):
                for k in range(KC):
                    last = nc.tensor.transpose(dst[:, k * P:(k + 1) * P], src[:, k * P:(k + 1) * P], ident)
                last.then_inc(s, 1)

            def times(dst, lhsT, rhs, s=None):
                for k in range(KC):
                    last = mm(dst, lhsT[:, k * P:(k + 1) * P], rhs(k), start=k == 0, stop=k == KC - 1)
                if s is not None:
                    last.then_inc(s, 1)

            def a_flip(r, u):
                pe.wait_ge(a_xn, r + 1)
                if not (static(r) and r < 2):
                    pe.wait_ge(a_xT, r - 1)
                flip(ps[u], xnb[:, u, :], a_xTp)

            def a_tile(r, u):
                if static(r) and r == 0:
                    a_flip(0, 0)
                if not (static(r) and r == T - 1):
                    a_flip(r + 1, 1 - u)
                pe.wait_ge(a_xT, r + 1)
                if not (static(r) and r < 2):
                    pe.wait_ge(a_kv, r - 1)
                times(ps[2 + u][:, :], xT[:, u, :], lambda k: wt[:, k, 0:512], a_qk)
                if not (static(r) and r == 0):
                    pe.wait_ge(a_kv, r)
                times(ps[4][:, 0:C], xT[:, u, :], lambda k: wt[:, k, 512:768])
                times(ps[4][:, C:C + E], xT[:, u, :], lambda k: wrt[:, k, :], a_vr)
                if not (static(r) and r == 0):
                    pe.wait_ge(a_h, r)
                times(ps[5][:, :], xT[:, u, :], lambda k: wgu[:, k, :], a_gu)
                if not (static(r) and r < 1):
                    a_hflip(r - 1, 1 - u)
                if not (static(r) and r < 2):
                    a_down(r - 2, u)

            def a_hflip(r, u):
                pe.wait_ge(a_h, r + 1)
                if not (static(r) and r < 1):
                    pe.wait_ge(a_hT, r)
                flip(ps[6], hb[:, u, :], a_hTp)

            def a_down(r, u):
                pe.wait_ge(a_hT, r + 1)
                if not (static(r) and r < 1):
                    pe.wait_ge(a_sh, r)
                times(ps[7][:, 0:C], hT[:, u, :], lambda k: wdn[:, k, :], a_dn)
            by_tile(pe, T, a_tile)
            a_down(T - 2, 0)
            a_hflip(T - 1, 1)
            a_down(T - 1, 1)

            pe.wait_ge(b_oh, 1)
            pe.wait_ge(a_hT, T)
            mm(ps[6][:, 0:256], tri, rt[:, 1, :], start=True, stop=True)
            mm(ps[6][:, 256:512], ones, rt[:, 1, :], start=True, stop=True).then_inc(b_cnt, 1)
            pe.wait_ge(b_tab, 1)
            pe.wait_ge(b_w, 16 * 3 * E)

            def b_flip(i, k):
                wait_turn(pe, b_in[k], i, 4)
                if not (static(i) and i < 2):
                    pe.wait_ge(b_xT, i - 1)
                flip(ps[k % 2], stage[:, k, :], b_xTp)

            def offset(i):
                return pe.value_load(etabi[0:1, bass.ds(i, 1)], min_val=0, max_val=(E - 1) * WEXP)

            def b_tile(i, k):
                u = k % 2
                if static(i) and i == 0:
                    b_flip(0, 0)
                if not (static(i) and i == NT - 1):
                    b_flip(i + 1, (k + 1) % 4)
                o = offset(i)
                pe.wait_ge(b_xT, i + 1)
                if not (static(i) and i < 2):
                    pe.wait_ge(b_h, i - 1)
                times(ps[2 + u][:, :], xT[:, u, :], lambda k: R[:, bass.ds(o + k * 2 * F, 2 * F)], b_gu)
                if not (static(i) and i < 1):
                    b_hflip(i - 1, 1 - u)
                if not (static(i) and i < 2):
                    b_down(i - 2, u)

            def b_hflip(i, u):
                pe.wait_ge(b_h, i + 1)
                if not (static(i) and i < 2):
                    pe.wait_ge(b_hT, i - 1)
                flip(ps[4 + u], hb[:, u, :], b_hTp)

            def b_down(i, u):
                o = offset(i)
                pe.wait_ge(b_hT, i + 1)
                if not (static(i) and i < 2):
                    pe.wait_ge(b_y, i - 1)
                times(ps[6 + u][:, 0:C], hT[:, u, :], lambda k: R[:, bass.ds(o + KC * 2 * F + k * C, C)], b_dn)
            by_tile(pe, NT, b_tile, 4)
            b_down(NT - 2, 0)
            b_hflip(NT - 1, 1)
            b_down(NT - 1, 1)

            def c_sums(r, u):
                pe.wait_ge(c_vd, r + 1)
                pe.wait_ge(c_vp, r + 1)
                if not (static(r) and r < 2):
                    pe.wait_ge(c_on, r - 1)
                for j in [*range(S0, NJ), *range(S0)]:
                    last = mm(ps[u][:, 0:C], ident, prodB[u][:, j, :], start=j == S0, stop=j == S0 - 1)
                last.then_inc(c_sum, 1)

            def c_proj(r, u):
                pe.wait_ge(c_on, r + 1)
                if not (static(r) and r < 1):
                    pe.wait_ge(c_oT, r)
                flip(ps[2], hb[:, u, :], c_oTp)
                pe.wait_ge(c_oT, r + 1)
                if not (static(r) and r < 2):
                    pe.wait_ge(c_out, r - 1)
                times(ps[3 + u][:, 0:C], hT[:, u, :], lambda k: wt[:, k, 768:1024], c_pr)

            def c_tile(r, u):
                c_sums(r, u)
                if not (static(r) and r < 1):
                    c_proj(r - 1, 1 - u)
            S0 = POOL_J
            by_tile(pe, T, c_tile)
            c_proj(T - 1, 1)


_INS = ["L0_attn_x", "L0_attn_qkv_w", "L0_attn_proj_w", "L0_attn_proj_b", "L0_ffn_router_w", "L0_ffn_gate_w",
        "L0_ffn_up_w", "L0_ffn_down_w", "L0_ffn_shared_gate_w", "L0_ffn_shared_up_w", "L0_ffn_shared_down_w"]


def kernel(**inputs):
    import numpy as _np
    import concourse.bacc as _bacc
    from concourse.bass_utils import run_bass_kernel_spmd as _run

    nc = _bacc.Bacc("TRN2", target_bir_lowering=False, num_devices=1)
    arrays, args = {}, []
    for name in _INS:
        a = _np.ascontiguousarray(inputs[name])
        if name == "L0_attn_x":
            a = a.reshape(BATCH * SEQ, C)
        arrays["in_" + name] = a
        args.append(nc.dram_tensor("in_" + name, a.shape, F32, kind="ExternalInput").ap())
    arrays["const"] = constants()
    args.append(nc.dram_tensor("const", (P, C_END), F32, kind="ExternalInput").ap())
    args.append(nc.dram_tensor("out_0", (BATCH * SEQ, C), F32, kind="ExternalOutput").ap())
    for name, shape in (("q_dram", (P, T, C)), ("shared_dram", (P, T, C)), ("gate_dram", (P, T, C)),
                        ("xs_dram", (NT * P, C)), ("ys_dram", (NT * P, C))):
        args.append(nc.dram_tensor(name, shape, F32, kind="Internal").ap())
    build(nc, *args)
    r = _run(nc, [arrays], core_ids=[0])
    return r.results[0]["out_0"].reshape(BATCH, SEQ, C)
```

```python
from contextlib import ExitStack

import numpy as np

import concourse.bass as bass
from concourse import mybir

F32 = mybir.dt.float32
F32R = mybir.dt.float32r
I32 = mybir.dt.int32
U32 = mybir.dt.uint32
ALU = mybir.AluOpType
ACT = mybir.ActivationFunctionType
AX = mybir.AxisListType.X

P = 128
BATCH, SEQ, C = 8, 512, 256
H, HD = 32, 8
WIN = 8
NJ = 2 * WIN
E, F = 8, 256
T = BATCH * SEQ // P
SEGS = SEQ // T
KC = C // P
HALO_L, HALO_R = WIN, WIN - 1
NPOS = T + HALO_L + HALO_R
NT = T + E
EPS = 1e-5
NEG = -3e38
ADDS, POOL_ADDS = (2, 1), (3,)
POOL_J, POOL_JL = 10, 10

BT = 2
BR = NT // BT
DT = 2
DR = BR + 1
END_CHUNKS = 2 * NJ // (4 * DT)

C_ID = 0
C_WJ = C_ID + P
C_EDGE = C_WJ + NJ * H
C_STAY = C_EDGE + 4 * WIN
C_TRI, C_ONE = C_STAY, C_STAY + P
C_FIRST = C_ONE + P
C_TILE = C_FIRST + E
C_END = C_TILE + NT


def constants():
    c = np.zeros((P, C_END), np.float32)
    c[:, C_ID:C_ID + P] = np.eye(P)
    c[:, C_TRI:C_TRI + P] = np.triu(np.ones((P, P)), 1)
    c[:, C_ONE:C_ONE + P] = 1.0
    d = np.abs(np.arange(NJ) - WIN).astype(np.float32)
    c[:, C_WJ:C_WJ + NJ * H] = np.repeat((WIN - d / 2.0) / WIN * np.float32(HD ** -0.5), H)
    p = np.arange(P)
    c[:, C_EDGE:C_EDGE + WIN] = np.where(p % SEGS == 0, NEG, 0.0)[:, None]
    c[:, C_EDGE + 3 * WIN:C_EDGE + 4 * WIN] = np.where(p % SEGS == SEGS - 1, NEG, 0.0)[:, None]
    c[:, C_FIRST:C_FIRST + E] = E - np.arange(E)
    c[:, C_TILE:C_TILE + NT] = np.arange(NT)
    return c


def static(t):
    return isinstance(t, int)


def place(s, wrapped=False):
    return (s + WIN) % T if static(s) else s + (WIN - T) if wrapped else s + WIN


def pairs(eng, lo, hi, body):
    with eng.Fori(lo // 2, hi // 2) as pair:
        for u in range(2):
            body(pair * 2 + u, u)


def by_tile(eng, n, body):
    body(0, 0)
    body(1, 1)
    pairs(eng, 2, n - 2, body)
    body(n - 2, 0)
    body(n - 1, 1)


def tiles_in(eng, lo, hi, body):
    if lo == 0:
        body(0, 0)
        body(1, 1)
    pairs(eng, max(lo, 2), hi, body)


def wait_turn(eng, sem, t, period=2):
    eng.wait_ge(sem, (t // period) * 16 + 16)


def wait_before(eng, sem, t, period=2):
    eng.wait_ge(sem, (t // period) * 16)


def wait_chunk(eng, sem, c, n):
    eng.wait_ge(sem, (c // 2) * (16 * n) + 16 * n)


def build(nc, x, qkv_w, proj_w, proj_b, router_w, gate_w, up_w, down_w, sgate_w, sup_w, sdown_w,
          const, out, q_dram, shared_dram, attn_dram, xs_dram, ys_dram):
    ctx = ExitStack()
    with ctx:
        def sb(name, shape, dt=F32):
            return ctx.enter_context(nc.sbuf_tensor(name, shape, dt))

        def sem(name):
            return ctx.enter_context(nc.semaphore(name))

        K = sb("K", [P, NPOS, C])
        V = sb("V", [P, NPOS, C])
        R = sb("R", [P, 2 * NJ * C])
        cst = sb("cst", [P, C_STAY])
        wproj = sb("wproj", [P, KC, C])
        pbias = sb("pbias", [1, C])
        bias = sb("bias", [1, 2, C], F32R)
        ones_r = sb("ones_r", [1, P], F32R)
        M = sb("M", [P, 2 * KC * 2 * F + 4 * KC * C + 4 * C + 5 * 2 * C])

        def cut(space):
            at = [0]

            def take(n):
                at[0] += n
                assert at[0] <= space.shape[1]
                return space[:, at[0] - n:at[0]]
            return take
        in_m = cut(M)
        egu = in_m(2 * KC * 2 * F).rearrange("p (b k f) -> p b k f", b=2, k=KC)
        edn = in_m(4 * KC * C).rearrange("p (b k c) -> p b k c", b=4, k=KC)
        stage = in_m(4 * C).rearrange("p (b c) -> p b c", b=4)
        xT, ga, hb, hT, yb = (in_m(2 * C).rearrange("p (b c) -> p b c", b=2) for _ in range(5))
        last_y, last_sh, last_s, last_x = (
            [a[:, (4 * b + k) * DT * C:(4 * b + k + 1) * DT * C] for a, n in ((M, 2), (R, END_CHUNKS)) for b in range(n)]
            for k in range(4))
        in_m = cut(M)
        rt = in_m(4 * T * E).rearrange("p (k c) -> p k c", k=4)
        lg = in_m(T * E).rearrange("p (t e) -> p t e", e=E)
        etab = in_m(NT * E).rearrange("p (t e) -> p t e", e=E)
        stats = in_m(6 * T).rearrange("p (t e) -> p t e", e=6)
        rcst = in_m(C_END - C_STAY)
        mv = in_m(8 * T).rearrange("p (k t) -> p k t", k=8)
        wrt = sb("wrt", [P, KC, E])
        q = sb("q", [P, 2, C])
        on = sb("on", [P, C])
        oT = sb("oT", [P, C])
        so = sb("so", [P, 2, C])
        xn = [q[:, :, :], so[:, :, :]]
        xT_n = [xT, ga]
        small = sb("small", [P, 2, NJ * H])
        mx = sb("mx", [P, 3, H])
        cnt = sb("cnt", [P, 5, E])
        cnti = sb("cnti", [P, E], I32)
        slot = sb("slot", [P, T], U32)
        etabs = sb("etabs", [P, NT])
        etabi = sb("etabi", [P, NT], I32)

        ident = cst[:, C_ID:C_ID + P]
        wj = cst[:, C_WJ:C_WJ + NJ * H]
        tri = rcst[:, C_TRI - C_STAY:C_TRI - C_STAY + P]
        ones = rcst[:, C_ONE - C_STAY:C_ONE - C_STAY + P]
        X = R[:, 0:T * C].rearrange("p (t c) -> p t c", c=C)
        raw = K[:, 0:8, :]
        raw_gu = K[:, 8:8 + KC * 2, :].rearrange("p a c -> p (a c)").rearrange("p (k f) -> p k f", k=KC)
        raw_dn = K[:, 8 + KC * 2:8 + KC * 3, :]
        prodA = [R[:, i * NJ * C:(i + 1) * NJ * C].rearrange("p (j c) -> p j c", c=C) for i in range(2)]
        with nc.sbuf_tensor("W", [P, 2 * NJ * C], F32R) as W:
            in_w = cut(W)
            weights = lambda n: [in_w(KC * n).rearrange("p (k f) -> p k f", k=KC) for _ in range(2)]
            wqkv, wgu, wdn = weights(3 * C), weights(2 * F), weights(C)
            xhi, xlo, hhi, hlo = (in_w(2 * C).rearrange("p (b c) -> p b c", b=2) for _ in range(4))
        PV = sb("PV", [P, 2 * NJ * C])
        prodB = [PV[:, i * NJ * C:(i + 1) * NJ * C].rearrange("p (j c) -> p j c", c=C) for i in range(2)]

        ps = [ctx.enter_context(nc.psum_tensor(f"ps{i}", [P, 512], F32)) for i in range(8)]

        XCH = 4
        SENDS = 4
        s_const, s_raw, s_wr, s_w, s_zero, s_fill = (
            sem("s_" + n) for n in ("const", "raw", "wr", "w", "zero", "fill"))
        s_x = [sem(f"s_x{i}") for i in range(XCH)]
        s_wtp, s_wtc, s_whi, s_wlo, s_dve, s_bn, s_var, s_sqrt = (
            sem("s_" + n) for n in ("wtp", "wtc", "whi", "wlo", "dve", "bn", "var", "sqrt"))
        n_xn, n_keep, n_xTp, n_xT, n_save, n_lg, n_lgc = (
            sem("n_" + n) for n in ("xn", "keep", "xTp", "xT", "save", "lg", "lgc"))
        a_xlo, a_hlo = sem("a_xlo"), sem("a_hlo")
        a_xT, a_qk, a_v, a_gu, a_silu, a_h, a_hTp, a_hT, a_dn, a_q, a_kv, a_sh = (
            sem("a_" + n) for n in ("xT", "qk", "v", "gu", "silu", "h", "hTp", "hT", "dn", "q", "kv", "sh"))
        a_qst, a_sst = ([sem(f"a_{n}{i}") for i in range(2)] for n in ("qst", "sst"))
        r_oh, r_cnt, r_sc, r_sce, r_tab, r_row = (
            sem("r_" + n) for n in ("oh", "cnt", "sc", "sce", "tab", "row"))
        r_scat = [sem(f"r_scat{i}") for i in range(SENDS)]
        b_in, b_wd = ([sem(f"b_{n}{i}") for i in range(4)] for n in ("in", "wd"))
        b_wg, b_st = ([sem(f"b_{n}{i}") for i in range(2)] for n in ("wg", "st"))
        b_xTp, b_xT, b_gu, b_silu, b_h, b_hTp, b_hT, b_dn, b_y = (
            sem("b_" + n) for n in ("xTp", "xT", "gu", "silu", "h", "hTp", "hT", "dn", "y"))
        c_vq, c_qk = sem("c_vq"), sem("c_qk")
        c_left, c_right = sem("c_left"), sem("c_right")
        c_q, c_sst = ([sem(f"c_{n}{i}") for i in range(2)] for n in ("q", "sst"))
        c_kp, c_kd, c_vp, c_vd, c_red, c_s, c_e, c_sum, c_on, c_oTp, c_oT, c_pr, c_so = (
            sem("c_" + n) for n in ("kp", "kd", "vp", "vd", "red", "s", "e", "sum", "on", "oTp", "oT", "pr", "so"))
        d_ld, d_y, d_st = ([sem(f"d_{n}{i}") for i in range(2 + END_CHUNKS)] for n in ("ld", "y", "st"))
        d_f, d_silu, d_s, d_o = (sem("d_" + n) for n in ("f", "silu", "s", "o"))

        x_v = x.rearrange("(p t) c -> p t c", t=T)
        out_v = out.rearrange("(p t) c -> p t c", t=T)
        NC = T // DT

        def adds(r, late=False):
            return () if late or (static(r) and r > DR) else ADDS

        def pool_adds(r, late=False):
            return () if late or (static(r) and r > DR) else POOL_ADDS

        QK0 = DR + 2
        QJ = 8

        def buffer_of(c):
            return c % 2 if c < NC - END_CHUNKS else 2 + c - (NC - END_CHUNKS)

        def in_so(c):
            return static(c) and c == NC - 1

        def wait_buffer(eng, sem, c, b, n):
            if b < 2:
                wait_chunk(eng, sem[b], c, n)
            else:
                eng.wait_ge(sem[b], 16 * n)

        def wait_place(eng, b):
            eng.wait_ge(c_red, T - 1 + (b - 2) // (END_CHUNKS // 2))

        def pool_offsets(r, late=False):
            return POOL_JL if late or (static(r) and r > DR) else POOL_J
        block = ctx.enter_context(nc.Block())

        def c_schedule(eng, tile):
            tile(0, 0)
            tile(1, 1)
            pairs(eng, 2, BR - 2, tile)
            for r in range(BR - 2, DR + 1):
                tile(r, r % 2)
            pairs(eng, DR + 1, T - 2, lambda r, u: tile(r, u, late=True))
            tile(T - 2, 0)
            tile(T - 1, 1)

        @block.sync
        def _(sp):
            n = T // XCH
            for i in range(XCH):
                sp.dma_start(X[:, i * n:(i + 1) * n, :], x_v[:, i * n:(i + 1) * n, :]).then_inc(s_x[i], 16)
                if i == 0:
                    sp.dma_start(cst[:, :], const[:, 0:C_STAY]).then_inc(s_const, 16)
                    sp.dma_start(rcst[:, :], const[:, C_STAY:C_END]).then_inc(s_const, 16)
                    sp.dma_start(raw[:, 0:6, :], qkv_w.rearrange("(a p) c -> p a c", p=P)).then_inc(s_raw, 16)
                    sp.dma_start(raw[:, 6:8, :], proj_w.rearrange("(a p) c -> p a c", p=P)).then_inc(s_raw, 16)
                    sp.dma_start(wrt[:, :, :], router_w.rearrange("(k p) f -> p k f", p=P)).then_inc(s_wr, 16)
            for dst, src in ((raw_gu[:, :, 0:F], sgate_w), (raw_gu[:, :, F:2 * F], sup_w), (raw_dn, sdown_w)):
                sp.dma_start(dst, src.rearrange("(k p) f -> p k f", p=P)).then_inc(s_w, 16)
            sp.dma_start(pbias[:, :], proj_b.unsqueeze(0)).then_inc(s_w, 16)
            sp.wait_ge(s_zero, 1)
            for i in range(NT // 4):
                sp.dma_start(xs_dram[i * 4 * P:(i + 1) * 4 * P, :].rearrange("(p r) c -> p r c", r=4),
                             small[:, :, :].rearrange("p a (b c) -> p (a b) c", c=C)).then_inc(s_fill, 16)

            def save(r, u):
                sp.wait_ge(a_q, r + 1)
                sp.dma_start(q_dram[:, bass.ds(r, 1), :], so[:, u:u + 1, :]).then_inc(a_qst[u], 16)
                if not (static(r) and r < 2):
                    save_shared(r - 2, u)

            def save_shared(r, u):
                sp.wait_ge(a_sh, r + 1)
                sp.dma_start(shared_dram[:, bass.ds(r, 1), :], yb[:, u:u + 1, :]).then_inc(a_sst[u], 16)

            def expert(i):
                return sp.value_load(etabi[0:1, bass.ds(i, 1)], min_val=0, max_val=E - 1)

            def load_gate_up(i, b):
                e = expert(i)
                if not (static(i) and i < 2):
                    sp.wait_ge(b_gu, i - 1)
                for w, c0 in ((gate_w, 0), (up_w, F)):
                    sp.dma_start(egu[:, b, :, c0:c0 + F],
                                 w[bass.ds(e, 1)].rearrange("e (k p) f -> p (e k) f", p=P)).then_inc(b_wg[b], 16)

            def load_down(i, b):
                e = expert(i)
                if not (static(i) and i < 4):
                    sp.wait_ge(b_dn, i - 3)
                sp.dma_start(edn[:, b, :, :],
                             down_w[bass.ds(e, 1)].rearrange("e (k p) c -> p (e k) c", p=P)).then_inc(b_wd[b], 16)

            def load_rows(i, b):
                if not (static(i) and i < 4):
                    sp.wait_ge(b_xTp, i - 3)
                sp.dma_start(stage[:, b, :], xs_dram[bass.ds(i * P, P), :]).then_inc(b_in[b], 16)

            def load_q(r, u, wrapped=False):
                if not (static(r) and r < 2):
                    sp.wait_ge(c_kd, r - 1)
                    sp.wait_ge(c_kp, r - 1)
                sp.dma_start(q[:, u:u + 1, :], q_dram[:, bass.ds(place(r, wrapped), 1), :]).then_inc(c_q[u], 16)

            save(0, 0)
            save(1, 1)
            pairs(sp, 2, WIN, save)
            sp.wait_ge(a_kv, HALO_R)
            for t in (K, V):
                sp.dma_start(t[0:P - 1, HALO_L + T:NPOS, :], t[1:P, HALO_L:HALO_L + HALO_R, :]).then_inc(c_right, 16)
                sp.dma_start(t[P - 1:P, HALO_L + T:NPOS, :], t[P - 1:P, HALO_L:HALO_L + HALO_R, :]).then_inc(c_right, 16)
            pairs(sp, WIN, T - WIN, save)
            for k in range(SENDS):
                sp.wait_ge(r_scat[k], 16 * (T // SENDS))
            sp.wait_ge(r_tab, 1)
            load_gate_up(0, 0)
            load_down(0, 0)
            for i in range(4):
                load_rows(i, i)
            for r in range(2):
                sp.wait_ge(a_qst[r], 16 * (place(r) // 2 + 1))
                load_q(r, r)
            load_gate_up(1, 1)
            pairs(sp, T - WIN, T - 2, save)
            save(T - 2, 0)
            save(T - 1, 1)
            save_shared(T - 2, 0)
            save_shared(T - 1, 1)

            def left_halo():
                for t in (K, V):
                    sp.dma_start(t[1:P, 0:HALO_L, :], t[0:P - 1, T:T + HALO_L, :]).then_inc(c_left, 16)
                    sp.dma_start(t[0:1, 0:HALO_L, :], t[0:1, T:T + HALO_L, :]).then_inc(c_left, 16)
            sp.wait_ge(a_kv, T)
            for u in range(2):
                sp.wait_ge(a_qst[u], 8 * T)

            def store_attention(r, u):
                sp.wait_ge(c_so, r + 1)
                sp.dma_start(attn_dram[:, bass.ds(r, 1), :], so[:, u:u + 1, :]).then_inc(c_sst[u], 16)

            def load_last(c, b):
                if static(c) and c == 0:
                    for u in range(2):
                        sp.wait_ge(a_sst[u], 8 * T)
                        sp.wait_ge(b_st[u], 8 * NT)
                if b >= 2:
                    wait_place(sp, b)
                elif not (static(c) and c < 2):
                    sp.wait_ge(d_o, c - 1)
                sources = [(last_sh, shared_dram, place(c * DT)), (last_x, x_v, place(c * DT))]
                if not in_so(c):
                    for u in range(2):
                        sp.wait_ge(c_sst[u], c * 16 + 16)
                    sources.append((last_s, attn_dram, c * DT))
                for dst, src, t in sources:
                    sp.dma_start(dst[b].rearrange("p (t c) -> p t c", t=DT), src[:, bass.ds(t, DT), :]).then_inc(d_ld[b], 16)

            def store_last(c, b):
                sp.wait_ge(d_o, c + 1)
                sp.dma_start(out_v[:, bass.ds(place(c * DT), DT), :], last_y[b].rearrange("p (t c) -> p t c", t=DT)).then_inc(d_st[b], 16)

            def c_tile(r, u, late=False):
                late = late or (static(r) and r >= DR)
                if not (static(r) and r >= T - 2):
                    load_q(r + 2, u, late)
                if static(r) and r == BR - 2:
                    left_halo()
                if not late and not (static(r) and r >= BR):
                    more = not (static(r) and r == BR - 1)
                    if more:
                        load_gate_up(r * 2 + 2, 0)
                    load_down(r * 2 + 1, 2 * u + 1)
                if not (static(r) and r < 2):
                    store_attention(r - 2, u)
                if not late and not (static(r) and r >= BR) and more:
                    load_gate_up(r * 2 + 3, 1)
                    load_down(r * 2 + 2, (2 * u + 2) % 4)
                    if not (static(r) and r == BR - 2):
                        load_rows(r * 2 + 4, 2 * u)
                        load_rows(r * 2 + 5, 2 * u + 1)
                if late and not (static(r) and r < DR + 1):
                    store_last(r - DR - 1, u)
                if late or (static(r) and r == DR - 1):
                    load_last(r - DR + 1, u)
            c_schedule(sp, c_tile)
            FIRST_END = T - DR
            for c in range(FIRST_END + 1, NC):
                load_last(c, buffer_of(c))
            store_last(FIRST_END - 1, buffer_of(FIRST_END - 1))
            for c in range(FIRST_END, NC):
                store_last(c, buffer_of(c))
            for b in range(2):
                sp.wait_ge(d_st[b], 8 * (NC - END_CHUNKS))
            for b in range(2, 2 + END_CHUNKS):
                sp.wait_ge(d_st[b], 16)

        @block.gpsimd
        def _(pool):
            nc.gpsimd.memset(small[:, :, :], 0.0).then_inc(s_zero, 1)

            def keep(t, u):
                pool.wait_ge(n_xn, t + 1)
                nc.gpsimd.tensor_copy(X[:, bass.ds(t * 2, 2), :], xn[u]).then_inc(n_keep, 1)
            by_tile(pool, T // 2, keep)
            pool.wait_ge(s_fill, 16 * (NT // 4))
            for t in range(T):
                pool.wait_ge(r_row, t // (T // SENDS) + 1)
                pool.indirect_dma_start(xs_dram, bass.IndirectOffsetOnAxis(ap=slot[:, t:t + 1], axis=0),
                                        X[:, t, :], None).then_inc(r_scat[t // (T // SENDS)], 16)
            for k in range(SENDS):
                pool.wait_ge(r_scat[k], 16 * (T // SENDS))

            def keys(r, u):
                wait_turn(pool, c_q[u], r)
                if static(r) and r == T - WIN:
                    pool.wait_ge(c_left, 16 * 4)
                if not (static(r) and r < 2):
                    pool.wait_ge(c_red, r - 1)
                n = pool_offsets(r)
                nc.gpsimd.tensor_tensor(
                    prodA[u][:, 0:n, :], K[:, bass.ds(place(r), n), :],
                    q[:, u, :].unsqueeze(1).broadcast_to([P, n, C]), ALU.mult).then_inc(c_kp, 1)

            def values(r, u):
                pool.wait_ge(c_e, r + 1)
                if static(r) and r == 0:
                    pool.wait_ge(a_dn, T)
                if not (static(r) and r < 2):
                    pool.wait_ge(c_sum, r - 1)
                n = pool_offsets(r)
                last = nc.gpsimd.tensor_tensor(
                    prodB[u][:, 0:n, :].rearrange("p j (h d) -> p j h d", d=HD),
                    V[:, bass.ds(place(r), n), :].rearrange("p j (h d) -> p j h d", d=HD),
                    small[:, u, 0:n * H].rearrange("p (j h) -> p j h", h=H).unsqueeze(3)
                    .broadcast_to([P, n, H, HD]), ALU.mult)
                for i, k in enumerate(pool_adds(r)):
                    last.then_inc(c_vq, 1)
                    pool.wait_ge(c_vq, r * len(POOL_ADDS) + i + 1)
                    last = nc.gpsimd.tensor_tensor(
                        prodB[u][:, 0:k, :], prodB[u][:, 0:k, :], prodB[u][:, n - k:n, :], ALU.add)
                    n -= k
                last.then_inc(c_vp, 1)

            def gather(c):
                b = buffer_of(c)
                if c == 0:
                    for u in range(2):
                        pool.wait_ge(b_st[u], 8 * NT)
                if b >= 2:
                    wait_place(pool, b)
                elif c >= 2:
                    pool.wait_ge(d_st[b], 16 * (c // 2))
                for k in range(DT):
                    t = place(c * DT + k)
                    pool.indirect_dma_start(last_y[b][:, k * C:(k + 1) * C], None, ys_dram,
                                            bass.IndirectOffsetOnAxis(ap=slot[:, t:t + 1], axis=0)).then_inc(d_y[b], 16)

            def c_tile(r, u):
                values(r, u)
                if static(r) and r >= DR:
                    gather(r - DR)
                if not (static(r) and r >= T - 2):
                    keys(r + 2, u)
            pool.wait_ge(a_kv, place(1) + WIN)
            keys(0, 0)
            keys(1, 1)
            pool.wait_ge(a_kv, T)
            pool.wait_ge(c_right, 16 * 4)
            c_tile(0, 0)
            c_tile(1, 1)
            pairs(pool, 2, BR, c_tile)
            for r in range(BR, T):
                c_tile(r, r % 2)
                if r == T - 2:
                    early = range(NC - END_CHUNKS, NC - END_CHUNKS // 2)
                    for c in early:
                        gather(c)
            for c in range(T - DR, NC):
                if c not in early:
                    gather(c)

        @block.scalar
        def _(act):
            def copy(dst, src):
                return nc.scalar.activation(dst, src, ACT.Copy)

            def weights(b):
                act.wait_ge(s_wtp, b + 1)
                dst = wqkv[0][:, :, b * 2 * P:(b + 1) * 2 * P] if b < 3 else wproj[:, :, :]
                copy(dst, ps[[2, 3, 6, 7][b]][:, :].rearrange("p (k c) -> p k c", k=KC)).then_inc(s_wtc, 1)

            def n_pair(t, u):
                act.wait_ge(n_xTp, t + 1)
                if not (static(t) and t < 2):
                    act.wait_ge(n_lg, t - 1)
                both = ps[u][:, :].rearrange("p (t c) -> p t c", c=C)
                copy(xT_n[u], both).then_inc(n_xT, 1)
                copy(V[:, bass.ds(t * 2 + HALO_L, 2), :], both).then_inc(n_save, 1)
            for b in range(4):
                weights(b)
            n = T // XCH
            for c in range(XCH):
                act.wait_ge(s_var, c + 1)
                nc.scalar.activation(mv[:, 2, c * n:(c + 1) * n], mv[:, 1, c * n:(c + 1) * n], ACT.Sqrt).then_inc(s_sqrt, 1)
                tiles_in(act, c * n // 2, (c + 1) * n // 2, n_pair)
                if c == 1:
                    act.wait_ge(s_w, 16 * 4)
                    copy(ones_r[:, :], ones[0:1, :])
                    copy(bias[:, 0, :], pbias[:, :])
                    copy(wgu[0], raw_gu)
                    copy(wdn[0], raw_dn).then_inc(s_whi, 1)
            act.wait_ge(n_lg, T // 2)

            def a_xcopy(r, u):
                if not (static(r) and r < 2):
                    act.wait_ge(a_gu, r - 1)
                copy(xhi[:, u:u + 1, :], V[:, bass.ds(r + HALO_L, 1), :]).then_inc(a_xT, 1)

            def a_tile(r, u):
                if static(r) and r == 0:
                    a_xcopy(0, 0)
                if not (static(r) and r == T - 1):
                    a_xcopy(r + 1, 1 - u)
                act.wait_ge(a_v, r + 1)
                if not (static(r) and r < 2):
                    wait_before(act, a_qst[u], r)
                copy(so[:, u, :], ps[2 + u][:, 0:C]).then_inc(a_q, 1)
                copy(K[:, bass.ds(r + HALO_L, 1), :], ps[2 + u][:, C:2 * C].unsqueeze(1))
                copy(V[:, bass.ds(r + HALO_L, 1), :], ps[4][:, 0:C].unsqueeze(1)).then_inc(a_kv, 1)
                act.wait_ge(a_gu, r + 1)
                if not (static(r) and r < 2):
                    act.wait_ge(a_h, r - 1)
                nc.scalar.activation(ga[:, u, :], ps[5][:, 0:F], ACT.Silu).then_inc(a_silu, 1)
                if not (static(r) and r < 1):
                    a_hcopy(r - 1, 1 - u)
                if not (static(r) and r < 2):
                    a_down(r - 2, u)

            def a_hcopy(r, u):
                act.wait_ge(a_hTp, r + 1)
                if not (static(r) and r < 2):
                    act.wait_ge(a_dn, r - 1)
                copy(hhi[:, u, :], ps[6][:, 0:F]).then_inc(a_hT, 1)

            def a_down(r, u):
                act.wait_ge(a_dn, r + 1)
                if not (static(r) and r < 2):
                    wait_before(act, a_sst[u], r)
                copy(yb[:, u, :], ps[7][:, 0:C]).then_inc(a_sh, 1)

            def c_exp(r, u):
                act.wait_ge(c_s, r + 1)
                nc.scalar.activation(small[:, u, :], small[:, u, :], ACT.Exp).then_inc(c_e, 1)

            act.wait_ge(n_keep, T // 2)
            act.wait_ge(n_save, T // 2)
            a_tile(0, 0)
            a_tile(1, 1)
            act.wait_ge(r_sc, 1)
            nc.scalar.activation(mv[:, 5, :], mv[:, 4, :], ACT.Sigmoid).then_inc(r_sce, 1)
            pairs(act, 2, T - 2, a_tile)
            a_tile(T - 2, 0)
            a_tile(T - 1, 1)
            a_down(T - 2, 0)
            a_hcopy(T - 1, 1)
            c_exp(0, 0)
            a_down(T - 1, 1)

            act.wait_ge(a_h, T)

            def b_xcopy(i, u):
                act.wait_ge(b_xTp, i + 1)
                if not (static(i) and i < 2):
                    act.wait_ge(b_gu, i - 1)
                copy(xT[:, u, :], ps[0][:, 0:C]).then_inc(b_xT, 1)

            def b_silu_of(i, u):
                act.wait_ge(b_gu, i + 1)
                if not (static(i) and i < 2):
                    act.wait_ge(b_h, i - 1)
                nc.scalar.activation(ga[:, u, :], ps[1 + u][:, 0:F], ACT.Silu).then_inc(b_silu, 1)

            def b_hcopy(i, u):
                act.wait_ge(b_hTp, i + 1)
                if not (static(i) and i < 2):
                    act.wait_ge(b_dn, i - 1)
                copy(hT[:, u, :], ps[3][:, 0:F]).then_inc(b_hT, 1)

            def b_rows(i, u):
                act.wait_ge(b_dn, i + 1)
                if static(i) and i < 2:
                    act.wait_ge(a_sst[u], 8 * T)
                else:
                    wait_before(act, b_st[u], i)
                copy(yb[:, u, :], ps[4][:, 0:C]).then_inc(b_y, 1)
                act.wait_ge(b_y, i + 1)
                act.dma_start(ys_dram[bass.ds(i * P, P), :], yb[:, u, :]).then_inc(b_st[u], 16)

            def c_ocopy(r):
                act.wait_ge(c_oTp, r + 1)
                copy(oT[:, :], ps[7][:, 0:C]).then_inc(c_oT, 1)

            def c_out(r, u):
                act.wait_ge(c_pr, r + 1)
                if static(r) and r < 2:
                    act.wait_ge(a_qst[u], 8 * T)
                else:
                    wait_before(act, c_sst[u], r)
                copy(so[:, u, :], ps[7][:, C:2 * C]).then_inc(c_so, 1)

            def d_silu_of(c, b):
                act.wait_ge(d_f, c + 1)
                nc.scalar.activation(last_sh[b], last_y[b], ACT.Silu).then_inc(d_silu, 1)

            def c_tile(r, u, late=False):
                late = late or (static(r) and r >= DR)
                experts = not late and not (static(r) and r >= BR)
                if experts:
                    b_xcopy(r * 2 + 1, 1)
                if not late and not (static(r) and r < 1):
                    b_hcopy(r * 2 - 2, 0)
                if experts:
                    b_silu_of(r * 2, 0)
                if not late and not (static(r) and r < 1):
                    b_rows(r * 2 - 2, 0)
                if not (static(r) and r < 2):
                    c_out(r - 2, u)
                if not (static(r) and r == T - 1):
                    c_exp(r + 1, 1 - u)
                if experts and not (static(r) and r == BR - 1):
                    b_xcopy(r * 2 + 2, 0)
                if not late and not (static(r) and r < 1):
                    b_hcopy(r * 2 - 1, 1)
                if experts:
                    b_silu_of(r * 2 + 1, 1)
                if not late and not (static(r) and r < 1):
                    b_rows(r * 2 - 1, 1)
                if not (static(r) and r < 1):
                    c_ocopy(r - 1)
                if late:
                    d_silu_of(r - DR, 1 - u)
            b_xcopy(0, 0)
            c_schedule(act, c_tile)
            c_out(T - 2, 0)
            c_ocopy(T - 1)
            c_out(T - 1, 1)
            for c in range(T - DR, NC):
                d_silu_of(c, buffer_of(c))

        @block.vector
        def _(dve):
            def chain(base):
                n = [0]

                def post(ins):
                    n[0] += 1
                    ins.then_inc(s_dve, 1)
                    return base + n[0]

                def step(ins):
                    dve.wait_ge(s_dve, post(ins))
                step.post = post
                return step, n
            tt, ts = nc.vector.tensor_tensor, nc.vector.tensor_scalar
            copy, reduce = nc.vector.tensor_copy, nc.vector.tensor_reduce
            step, at = chain(0)

            def normalise(t, u, ahead):
                if not (static(t) and t < 2):
                    dve.wait_ge(n_xTp, t - 1)
                    dve.wait_ge(n_keep, t - 1)
                for i in range(2):
                    ins = ts(xn[u][:, i:i + 1, :], X[:, bass.ds(t * 2 + i, 1), :], mv[:, 0, bass.ds(t * 2 + i, 1)],
                             mv[:, 6, bass.ds(t * 2 + i, 1)], ALU.subtract, ALU.mult)
                ins.then_inc(n_xn, 1)
                if ahead:
                    moments(t + ahead)
                if not (static(t) and t < 2):
                    logits(t - 2, u)

            def moments(t):
                for i in range(2):
                    nc.vector.bn_stats(stats[:, bass.ds(t * 2 + i, 1), :], X[:, bass.ds(t * 2 + i, 1), :]).then_inc(s_bn, 1)

            def logits(t, u):
                dve.wait_ge(n_lg, t + 1)
                copy(lg[:, bass.ds(t * 2, 2), :], ps[4 + u][:, 0:2 * E].rearrange("p (t e) -> p t e", e=E)).then_inc(n_lgc, 1)

            for c in range(XCH):
                n = T // XCH
                lo = slice(c * n, (c + 1) * n)
                if c == 0:
                    dve.wait_ge(s_x[0], 16)
                    pairs(dve, 0, n // 2, lambda t, u: moments(t))
                dve.wait_ge(s_bn, n * (c + 1))
                me, m2e, mo, m2o = (stats[:, lo, k] for k in (1, 2, 4, 5))
                m = lambda k: mv[:, k, lo]
                tt(m(0), me, mo, ALU.add)
                tt(m(3), me, mo, ALU.subtract)
                step(tt(m(4), m2e, m2o, ALU.add))
                ts(m(0), m(0), 0.5, None, ALU.mult)
                step(tt(m(3), m(3), m(3), ALU.mult))
                step(ts(m(4), m(4), 1.0 / C, EPS, ALU.mult, ALU.add))
                step(ts(m(3), m(3), 0.25, None, ALU.mult))
                step(tt(m(1), m(3), m(4), ALU.add))
                copy(m(7), m(1)).then_inc(s_var, 1)
                dve.wait_ge(s_sqrt, c + 1)
                step(nc.vector.reciprocal(m(3), m(2)))
                step(tt(m(3), m(3), m(1), ALU.mult))
                step(tt(m(3), m(3), m(2), ALU.add))
                step(ts(m(3), m(3), 0.5, None, ALU.mult))
                step(nc.vector.reciprocal(m(6), m(3)))
                if c < XCH - 1:
                    dve.wait_ge(s_x[c + 1], 16)
                ahead = n // 2 if c < XCH - 1 else 0
                tiles_in(dve, c * n // 2, (c + 1) * n // 2, lambda t, u: normalise(t, u, ahead))
                if c == 0:
                    for b in range(3):
                        dve.wait_ge(s_wtc, b + 1)
                        block_b = slice(b * 2 * P, (b + 1) * 2 * P)
                        tt(wqkv[1][:, :, block_b], ps[[2, 3, 6][b]][:, :].rearrange("p (k c) -> p k c", k=KC),
                           wqkv[0][:, :, block_b].bitcast(F32), ALU.subtract).then_inc(s_wlo, 1)
                if c == 2:
                    dve.wait_ge(s_whi, 1)
                    tt(wgu[1], raw_gu, wgu[0].bitcast(F32), ALU.subtract).then_inc(s_wlo, 1)
                    tt(wdn[1], raw_dn, wdn[0].bitcast(F32), ALU.subtract).then_inc(s_wlo, 1)
                    tt(bias[:, 1, :], pbias[:, :], bias[:, 0, :].bitcast(F32), ALU.subtract).then_inc(s_wlo, 1)
            logits(T // 2 - 2, 0)
            logits(T // 2 - 1, 1)

            def swiglu(r, u, gu, s_gate, s_h, free):
                dve.wait_ge(s_gate, r + 1)
                if not (static(r) and r < 2):
                    dve.wait_ge(free, r - 1)
                tt(hb[:, u, :], gu[:, F:2 * F], ga[:, u, :], ALU.mult).then_inc(s_h, 1)

            v3 = lambda k: rt[:, k, :].rearrange("p (t e) -> p t e", e=E)

            def choose(step):
                dve.wait_ge(n_lgc, T // 2)
                step(reduce(mv[:, 4, :], lg[:, :, :], AX, ALU.max))
                copy(mv[:, 7, :], mv[:, 4, :]).then_inc(r_sc, 1)
                step(tt(v3(0), lg[:, :, :], mv[:, 4, :].unsqueeze(2).broadcast_to([P, T, E]), ALU.is_ge))
                first = rcst[:, C_FIRST - C_STAY:C_FIRST - C_STAY + E].unsqueeze(1).broadcast_to([P, T, E])
                step(tt(v3(0), v3(0), first, ALU.mult))
                step(reduce(mv[:, 3, :], v3(0), AX, ALU.max))
                tt(v3(1), first, mv[:, 3, :].unsqueeze(2).broadcast_to([P, T, E]), ALU.is_equal).then_inc(r_oh, 1)

            def rank(step):
                dve.wait_ge(r_cnt, 1)
                step(copy(rt[:, 2, :], ps[1][:, 0:T * E]))
                for e in range(E):
                    ins = nc.vector.tensor_tensor_scan(v3(3)[:, :, e], ones[:, 0:T], v3(2)[:, :, e], 0.0, ALU.mult, ALU.add)
                step(ins)

            def tiles_of(step):
                step(copy(cnt[:, 0, :], v3(3)[:, T - 1, :]))
                step(ts(cnt[:, 1, :], cnt[:, 0, :], float(P - 1), None, ALU.add))
                step(copy(cnti[:, :], cnt[:, 1, :]))
                step(ts(cnti[:, :], cnti[:, :], 7, None, ALU.arith_shift_right))
                step(copy(cnt[:, 2, :], cnti[:, :]))
                step(nc.vector.tensor_tensor_scan(cnt[:, 3, :], ones[:, 0:E], cnt[:, 2, :], 0.0, ALU.mult, ALU.add))
                step(tt(cnt[:, 4, :], cnt[:, 3, :], cnt[:, 2, :], ALU.subtract))
                step(ts(cnt[:, 4, :], cnt[:, 4, :], float(P), None, ALU.mult))

            def slots(step):
                step(tt(rt[:, 3, :], rt[:, 3, :], rt[:, 2, :], ALU.subtract))
                step(tt(rt[:, 3, :], rt[:, 3, :], ps[0][:, 0:T * E], ALU.add))
                step(tt(v3(3), v3(3), cnt[:, 4, :].unsqueeze(1).broadcast_to([P, T, E]), ALU.add))
                step(tt(rt[:, 3, :], rt[:, 3, :], rt[:, 1, :], ALU.mult))
                step(reduce(mv[:, 3, :], v3(3), AX, ALU.add))
                step(copy(slot[:, :], mv[:, 3, :]))

            def scale(k):
                n = T // SENDS
                if k == 0:
                    dve.wait_ge(r_sce, 1)
                    dve.wait_ge(n_keep, T // 2)
                tt(X[:, k * n:(k + 1) * n, :], X[:, k * n:(k + 1) * n, :],
                   mv[:, 5, k * n:(k + 1) * n].unsqueeze(2).broadcast_to([P, n, C]), ALU.mult).then_inc(r_row, 1)

            def table(step):
                step(tt(etab[:, :, :], rcst[:, C_TILE - C_STAY:C_TILE - C_STAY + NT].unsqueeze(2).broadcast_to([P, NT, E]),
                        cnt[:, 3, :].unsqueeze(1).broadcast_to([P, NT, E]), ALU.is_ge))
                step(reduce(etabs[:, :], etab[:, :, :], AX, ALU.add))
                step(ts(etabs[:, :], etabs[:, :], float(E - 1), None, ALU.min))
                copy(etabi[:, :], etabs[:, :]).then_inc(r_tab, 1)

            def x_low(r, u):
                dve.wait_ge(a_xT, r + 1)
                if not (static(r) and r < 2):
                    dve.wait_ge(a_gu, r - 1)
                tt(xlo[:, u:u + 1, :], V[:, bass.ds(r + HALO_L, 1), :], xhi[:, u:u + 1, :].bitcast(F32), ALU.subtract).then_inc(a_xlo, 1)

            def h_low(r, u):
                dve.wait_ge(a_hT, r + 1)
                if not (static(r) and r < 2):
                    dve.wait_ge(a_dn, r - 1)
                tt(hlo[:, u, :], ps[6][:, 0:F], hhi[:, u, :].bitcast(F32), ALU.subtract).then_inc(a_hlo, 1)

            def a_tile(r, u):
                if not (static(r) and r == T - 1):
                    x_low(r + 1, 1 - u)
                swiglu(r, u, ps[5], a_silu, a_h, a_hTp)
                if not (static(r) and r < 1):
                    h_low(r - 1, 1 - u)
            x_low(0, 0)
            parts = [choose, rank, tiles_of, slots] + [scale] * SENDS + [table]
            A1 = 1 + len(parts)
            a_tile(0, 0)
            for r, part in enumerate(parts, 1):
                if part is scale:
                    scale(r - 1 - parts.index(scale))
                else:
                    part(step)
                a_tile(r, r % 2)
            pairs(dve, A1, T - WIN // 2, a_tile)
            base_c = at[0]

            def keys(r, u, late=False):
                wait_turn(dve, c_q[u], r)
                if static(r) and r == T - WIN:
                    dve.wait_ge(c_left, 16 * 4)
                j0 = pool_offsets(r, late)
                tt(prodA[u][:, j0:NJ, :], K[:, bass.ds(place(r, late) + j0, NJ - j0), :],
                   q[:, u, :].unsqueeze(1).broadcast_to([P, NJ - j0, C]), ALU.mult).then_inc(c_kd, 1)

            def scores(r, u, step, edge, late=False, between=(), before_last=()):
                dve.wait_ge(c_kp, r + 1)
                dve.wait_ge(c_kd, r + 1)
                if not (static(r) and r < 2):
                    dve.wait_ge(c_vp, r - 1)
                s = small[:, u, :]
                s3 = s.rearrange("p (j h) -> p j h", h=H)
                for_j = s.rearrange("p (j h) -> p h j", h=H)
                jn = NJ
                if late or (static(r) and r >= QK0):
                    dve.wait_ge(c_qk, r + (1 - QK0))
                    jn = QJ
                reduce(s3[:, 0:jn, :], prodA[u][:, 0:jn, :].rearrange("p j (h d) -> p j h d", d=HD), AX, ALU.add).then_inc(c_red, 1)
                if jn < NJ:
                    tt(s[:, jn * H:], ps[u][:, 0:(NJ - jn) * H], wj[:, jn * H:], ALU.mult)
                dve.wait_ge(c_red, r + 1)
                weighed = step.post(tt(s[:, 0:jn * H], s[:, 0:jn * H], wj[:, 0:jn * H], ALU.mult))
                for other in between:
                    other()
                dve.wait_ge(s_dve, weighed)
                if edge is not None:
                    e0 = C_EDGE if edge == "first" else C_EDGE + 2 * WIN + WIN - T
                    half = s3[:, 0:WIN, :] if edge == "first" else s3[:, WIN:NJ, :]
                    step(tt(half, half, cst[:, bass.ds(place(r, late) + e0, WIN)].unsqueeze(2).broadcast_to([P, WIN, H]), ALU.add))
                largest = step.post(reduce(mx[:, 0, :], for_j, AX, ALU.max))
                for other in before_last:
                    other()
                dve.wait_ge(s_dve, largest)
                tt(s3, s3, mx[:, 0, :].unsqueeze(1).broadcast_to([P, NJ, H]), ALU.subtract).then_inc(c_s, 1)

            def values(r, u, step, late):
                dve.wait_ge(c_e, r + 1)
                if static(r) and r == 0:
                    dve.wait_ge(a_dn, T)
                if not (static(r) and r < 2):
                    dve.wait_ge(c_sum, r - 1)
                j0 = pool_offsets(r, late)
                product = tt(
                    prodB[u][:, j0:NJ, :].rearrange("p j (h d) -> p j h d", d=HD),
                    V[:, bass.ds(place(r, late) + j0, NJ - j0), :].rearrange("p j (h d) -> p j h d", d=HD),
                    small[:, u, j0 * H:].rearrange("p (j h) -> p j h", h=H).unsqueeze(3)
                    .broadcast_to([P, NJ - j0, H, HD]), ALU.mult)
                todo = list(adds(r, late))
                if todo:
                    summed = step.post(product)
                else:
                    product.then_inc(c_vd, 1)
                if not (static(r) and r < 2):
                    dve.wait_ge(c_on, r - 1)
                total = step.post(reduce(mx[:, 1 + u, :], small[:, u, :].rearrange("p (j h) -> p h j", h=H), AX, ALU.add))

                def add(n, end):
                    dve.wait_ge(s_dve, summed)
                    return tt(prodB[u][:, j0:j0 + n, :], prodB[u][:, j0:j0 + n, :], prodB[u][:, end - n:end, :], ALU.add)
                end = NJ
                while len(todo) > 1:
                    n = todo.pop(0)
                    summed = step.post(add(n, end))
                    end -= n
                dve.wait_ge(s_dve, total)
                inverse = step.post(nc.vector.reciprocal(mx[:, 1 + u, :], mx[:, 1 + u, :]))
                if static(r) and r == T - 1:
                    dve.wait_ge(s_dve, inverse)
                if todo:
                    add(todo[0], end).then_inc(c_vd, 1)

            def attend(r, u):
                dve.wait_ge(c_sum, r + 1)
                if not (static(r) and r < 1):
                    dve.wait_ge(c_oTp, r)
                tt(on[:, :].rearrange("p (h d) -> p h d", d=HD),
                   ps[5 + u][:, 0:C].rearrange("p (h d) -> p h d", d=HD),
                   mx[:, 1 + u, :].unsqueeze(2).broadcast_to([P, H, HD]), ALU.mult).then_inc(c_on, 1)

            def d_sum(c, b):
                wait_buffer(dve, d_y, c, b, DT)
                wait_buffer(dve, d_ld, c, b, 2 if in_so(c) else 3)
                tt(last_y[b], last_y[b], last_sh[b], ALU.add).then_inc(d_f, 1)

            def d_out(c, b):
                dve.wait_ge(d_silu, c + 1)
                if in_so(c):
                    dve.wait_ge(c_so, T)
                attention = so[:, :, :].rearrange("p t c -> p (t c)") if in_so(c) else last_s[b]
                tt(last_y[b], last_sh[b], attention, ALU.mult).then_inc(d_s, 1)
                dve.wait_ge(d_s, c + 1)
                tt(last_y[b], last_y[b], last_x[b], ALU.add).then_inc(d_o, 1)

            def c_tile(r, u, step, edge, late=False):
                wrapped = late and not static(r)
                late = late or (static(r) and r >= DR)
                values(r, u, step, wrapped)
                if not late and not (static(r) and r < 1):
                    swiglu(r * 2 - 1, 1, ps[2], b_silu, b_h, b_hTp)
                if late and not (static(r) and r == DR):
                    d_out(r - DR - 1, u)
                between, before_last = [], []
                if not (static(r) and r < 1):
                    (between if late else before_last).append(lambda: attend(r - 1, 1 - u))
                if not late and not (static(r) and r >= BR):
                    between.append(lambda: swiglu(r * 2, 0, ps[1], b_silu, b_h, b_hTp))
                if not (static(r) and r == T - 1):
                    scores(r + 1, 1 - u, step, edge, wrapped, between, before_last)
                else:
                    attend(r - 1, 1 - u)
                if late:
                    d_sum(r - DR, 1 - u)
                if not (static(r) and r >= T - 2):
                    keys(r + 2, u, wrapped)

            for k in range(SENDS):
                dve.wait_ge(r_scat[k], 16 * (T // SENDS))
            dve.wait_ge(a_kv, place(1) + WIN)
            keys(0, 0)
            a_tile(T - 4, 0)
            keys(1, 1)
            a_tile(T - 3, 1)
            step, at = chain(base_c)
            scores(0, 0, step, None, between=[lambda: a_tile(T - 2, 0)], before_last=[lambda: a_tile(T - 1, 1)])
            h_low(T - 1, 1)
            dve.wait_ge(a_hTp, T)
            dve.wait_ge(a_kv, T)
            dve.wait_ge(c_right, 16 * 4)
            for r in range(2):
                c_tile(r, r, step, None)
            steps = base_c + at[0]

            def alone(steps, *tiles):
                step, at = chain(steps)
                for r, edge in tiles:
                    c_tile(r, r % 2, step, edge)
                return steps + at[0]

            def run(steps, lo, hi, edge, late):
                per = 4 + (0 if late else len(ADDS)) + (edge is not None)

                def tile(r, u):
                    step, at = chain((r - lo) * per + steps)
                    c_tile(r, u, step, edge, late)
                    assert at[0] == per
                pairs(dve, lo, hi, tile)
                return steps + per * (hi - lo)
            LAST = T - HALO_R - WIN - 1
            steps = run(steps, 2, LAST, None, False)
            steps = run(steps, LAST, BR, "last", False)
            steps = alone(steps, *((r, "last" if r + 1 < T - WIN else "first") for r in range(BR, T - WIN)))
            steps = run(steps, T - WIN, T - 2, "first", True)
            step, at = chain(steps)
            c_tile(T - 2, 0, step, "first")
            c_tile(T - 1, 1, step, None)
            attend(T - 1, 1)
            d_out(T - DR - 1, buffer_of(T - DR - 1))
            d_sum(T - DR, buffer_of(T - DR))
            d_sum(T - DR + 1, buffer_of(T - DR + 1))
            for c in range(T - DR, NC):
                if c + 2 < NC:
                    d_sum(c + 2, buffer_of(c + 2))
                d_out(c, buffer_of(c))

        @block.tensor
        def _(pe):
            mm = nc.tensor.matmul

            def flip(dst, src, s):
                for k in range(KC):
                    last = nc.tensor.transpose(dst[:, k * P:(k + 1) * P], src[:, k * P:(k + 1) * P], ident)
                last.then_inc(s, 1)

            def times(dst, lhsT, rhs, s=None):
                for k in range(KC):
                    last = mm(dst, lhsT[:, k * P:(k + 1) * P], rhs(k), start=k == 0, stop=k == KC - 1)
                if s is not None:
                    last.then_inc(s, 1)

            pe.wait_ge(s_const, 32)
            pe.wait_ge(s_raw, 32)
            for b in range(4):
                for kc in range(KC):
                    for a in range(2):
                        last = nc.tensor.transpose(ps[[2, 3, 6, 7][b]][:, (2 * kc + a) * P:(2 * kc + a + 1) * P],
                                                   raw[:, 2 * b + a, kc * P:(kc + 1) * P], ident)
                last.then_inc(s_wtp, 1)

            def n_flip(t, u):
                pe.wait_ge(n_xn, t + 1)
                if not (static(t) and t < 2):
                    pe.wait_ge(n_save, t - 1)
                for i in range(2 * KC):
                    last = nc.tensor.transpose(ps[u][:, i * P:(i + 1) * P],
                                               xn[u][:, i // KC, i % KC * P:(i % KC + 1) * P], ident)
                last.then_inc(n_xTp, 1)

            def n_pair(t, u):
                n_flip(t, u)
                if not (static(t) and t < 1):
                    n_router(t - 1, 1 - u)

            def n_router(t, u):
                pe.wait_ge(n_xT, t + 1)
                if not (static(t) and t < 2):
                    pe.wait_ge(n_lgc, t - 1)
                times(ps[4 + u][:, 0:E], xT_n[u][:, 0, :], lambda k: wrt[:, k, :])
                times(ps[4 + u][:, E:2 * E], xT_n[u][:, 1, :], lambda k: wrt[:, k, :], n_lg)
            pe.wait_ge(s_wr, 16)
            by_tile(pe, T // 2, n_pair)
            n_router(T // 2 - 1, 1)
            pe.wait_ge(s_wtc, 4)
            pe.wait_ge(s_wlo, 6)
            pe.wait_ge(n_lgc, T // 2)
            pe.wait_ge(n_save, T // 2)

            def times3(dst, hi, lo, w, cols, s, wait_lo=None):
                parts = [(hi, w[0]), (hi, w[1]), (lo, w[0])]
                for i, (x_, w_) in enumerate(parts):
                    if i == 2 and wait_lo:
                        wait_lo()
                    for k in range(KC):
                        last = mm(dst, x_[:, k * P:(k + 1) * P], w_[:, k, cols],
                                  start=i == 0 and k == 0, stop=i == 2 and k == KC - 1)
                last.then_inc(s, 1)

            def a_tile(r, u):
                pe.wait_ge(a_xT, r + 1)
                if not (static(r) and r < 2):
                    pe.wait_ge(a_kv, r - 1)
                times3(ps[2 + u][:, :], xhi[:, u, :], xlo[:, u, :], wqkv, slice(0, 2 * C), a_qk,
                       lambda: pe.wait_ge(a_xlo, r + 1))
                if not (static(r) and r == 0):
                    pe.wait_ge(a_kv, r)
                times3(ps[4][:, 0:C], xhi[:, u, :], xlo[:, u, :], wqkv, slice(2 * C, 3 * C), a_v)
                if not (static(r) and r == 0):
                    pe.wait_ge(a_h, r)
                times3(ps[5][:, :], xhi[:, u, :], xlo[:, u, :], wgu, slice(0, 2 * F), a_gu)
                if not (static(r) and r < 1):
                    a_hflip(r - 1, 1 - u)
                if not (static(r) and r < 2):
                    a_down(r - 2, u)

            def a_hflip(r, u):
                pe.wait_ge(a_h, r + 1)
                if not (static(r) and r < 1):
                    pe.wait_ge(a_hlo, r)
                flip(ps[6], hb[:, u, :], a_hTp)

            def a_down(r, u):
                pe.wait_ge(a_hT, r + 1)
                if not (static(r) and r < 1):
                    pe.wait_ge(a_sh, r)
                times3(ps[7][:, 0:C], hhi[:, u, :], hlo[:, u, :], wdn, slice(0, C), a_dn,
                       lambda: pe.wait_ge(a_hlo, r + 1))
            a_tile(0, 0)
            a_tile(1, 1)
            pe.wait_ge(r_oh, 1)
            mm(ps[0][:, 0:T * E], tri, rt[:, 1, :], start=True, stop=True)
            mm(ps[1][:, 0:T * E], ones, rt[:, 1, :], start=True, stop=True).then_inc(r_cnt, 1)
            pairs(pe, 2, T - 2, a_tile)
            a_tile(T - 2, 0)
            a_tile(T - 1, 1)
            a_down(T - 2, 0)
            a_hflip(T - 1, 1)
            a_down(T - 1, 1)
            pe.wait_ge(r_row, SENDS)
            pe.wait_ge(a_kv, T)
            pe.wait_ge(a_h, T)
            pe.wait_ge(a_hlo, T)
            pe.wait_ge(a_sh, T)

            def b_flip(i, b):
                wait_turn(pe, b_in[b], i, 4)
                if not (static(i) and i < 1):
                    pe.wait_ge(b_xT, i)
                flip(ps[0], stage[:, b, :], b_xTp)

            def b_gate_up(i, b):
                pe.wait_ge(b_xT, i + 1)
                wait_chunk(pe, b_wg[b % 2], i, 2)
                if not (static(i) and i < 2):
                    pe.wait_ge(b_h, i - 1)
                times(ps[1 + b % 2][:, :], xT[:, b % 2, :], lambda k: egu[:, b % 2, k, :], b_gu)

            def b_hflip(i, b):
                pe.wait_ge(b_h, i + 1)
                if not (static(i) and i < 1):
                    pe.wait_ge(b_hT, i)
                flip(ps[3], hb[:, b % 2, :], b_hTp)

            def b_down(i, b):
                pe.wait_ge(b_hT, i + 1)
                wait_turn(pe, b_wd[b], i, 4)
                if not (static(i) and i < 1):
                    pe.wait_ge(b_y, i)
                times(ps[4][:, 0:C], hT[:, b % 2, :], lambda k: edn[:, b, k, :], b_dn)

            def b_step(i, b, more, ends):
                if more:
                    b_flip(i + 1, (b + 1) % 4)
                if not (static(i) and i < 2):
                    b_hflip(i - 2, (b + 2) % 4)
                if not ends:
                    b_gate_up(i, b)
                if not (static(i) and i < 2):
                    b_down(i - 2, (b + 2) % 4)

            def c_qk_sums(r, u):
                pe.wait_ge(c_kd, r + 1)
                pe.wait_ge(c_kp, r + 1)
                pe.wait_ge(c_s, r - 1)
                n = (NJ - QJ) * H
                by_d = prodA[u][:, QJ:NJ, :].rearrange("p j (h d) -> p d (j h)", d=HD)
                for d in range(HD):
                    last = mm(ps[u][:, 0:n], ident, by_d[:, d, :], start=d == 0, stop=d == HD - 1)
                last.then_inc(c_qk, 1)

            def c_sums(r, u, late):
                pe.wait_ge(c_vd, r + 1)
                if not (static(r) and r < 2):
                    pe.wait_ge(c_on, r - 1)
                j0 = pool_offsets(r, late)
                for j in range(j0, NJ - sum(adds(r, late))):
                    mm(ps[5 + u][:, 0:C], ident, prodB[u][:, j, :], start=j == j0, stop=False)
                pe.wait_ge(c_vp, r + 1)
                n = j0 - sum(pool_adds(r, late))
                for j in range(n):
                    last = mm(ps[5 + u][:, 0:C], ident, prodB[u][:, j, :], start=False, stop=j == n - 1)
                last.then_inc(c_sum, 1)

            def c_flip(r):
                pe.wait_ge(c_on, r + 1)
                if not (static(r) and r < 1):
                    pe.wait_ge(c_so, r)
                flip(ps[7], on[:, :], c_oTp)

            def c_proj(r):
                pe.wait_ge(c_oT, r + 1)
                for k in range(2):
                    mm(ps[7][:, C:2 * C], ones_r[:, :], bias[:, k, :], start=k == 0, stop=False)
                for k in range(KC):
                    last = mm(ps[7][:, C:2 * C], oT[:, k * P:(k + 1) * P], wproj[:, k, :], start=False, stop=k == KC - 1)
                last.then_inc(c_pr, 1)

            def c_tile(r, u, late=False):
                late = late or (static(r) and r >= DR)
                ends = static(r) and r == BR
                if late and not (static(r) and (r < QK0 - 1 or r == T - 1)):
                    c_qk_sums(r + 1, 1 - u)
                if not late:
                    b_step(r * 2, 2 * u, not ends, ends)
                if not (static(r) and r < 2):
                    c_proj(r - 2)
                c_sums(r, u, late and not static(r))
                if not late:
                    b_step(r * 2 + 1, 2 * u + 1, not (static(r) and r >= BR - 1), ends)
                if not (static(r) and r < 1):
                    c_flip(r - 1)
            b_flip(0, 0)
            c_schedule(pe, c_tile)
            c_proj(T - 2)
            c_flip(T - 1)
            c_proj(T - 1)


_INS = ["L0_attn_x", "L0_attn_qkv_w", "L0_attn_proj_w", "L0_attn_proj_b", "L0_ffn_router_w", "L0_ffn_gate_w",
        "L0_ffn_up_w", "L0_ffn_down_w", "L0_ffn_shared_gate_w", "L0_ffn_shared_up_w", "L0_ffn_shared_down_w"]


def kernel(**inputs):
    import numpy as _np
    import concourse.bacc as _bacc
    from concourse.bass_utils import run_bass_kernel_spmd as _run

    nc = _bacc.Bacc("TRN2", target_bir_lowering=False, num_devices=1)
    arrays, args = {}, []
    for name in _INS:
        a = _np.ascontiguousarray(inputs[name])
        if name == "L0_attn_x":
            a = a.reshape(BATCH * SEQ, C)
        arrays["in_" + name] = a
        args.append(nc.dram_tensor("in_" + name, a.shape, F32, kind="ExternalInput").ap())
    arrays["const"] = constants()
    args.append(nc.dram_tensor("const", (P, C_END), F32, kind="ExternalInput").ap())
    args.append(nc.dram_tensor("out_0", (BATCH * SEQ, C), F32, kind="ExternalOutput").ap())
    for name, shape in (("q_dram", (P, T, C)), ("shared_dram", (P, T, C)), ("attn_dram", (P, T, C)),
                        ("xs_dram", (NT * P, C)), ("ys_dram", (NT * P, C))):
        args.append(nc.dram_tensor(name, shape, F32, kind="Internal").ap())
    build(nc, *args)
    r = _run(nc, [arrays], core_ids=[0])
    return r.results[0]["out_0"].reshape(BATCH, SEQ, C)
```
